# Optimizing a Trainium2 kernel written in Bass

```python
import numpy as np
import jax
import jax.numpy as jnp

def _softmax(x, axis=-1):
    return jax.nn.softmax(x, axis=axis)

def _gelu(x):
    return jax.nn.gelu(x, approximate=True)

def _silu(x):
    return jax.nn.silu(x)

def _sigmoid(x):
    return jax.nn.sigmoid(x)

def _layernorm(x, axis=-1, eps=1e-05):
    m = jnp.mean(x, axis=axis, keepdims=True)
    v = jnp.var(x, axis=axis, keepdims=True)
    return (x - m) / jnp.sqrt(v + eps)

def _scatter_add(tgt, idx, src, axis=0):
    return tgt.at[idx].add(src)

def _segment_sum(src, seg, n):
    return jax.ops.segment_sum(src, seg, n)
kernel_name = 'mk_xattn_ffn_d1_seqx_r8_a39991'

def setup_inputs(seed: int=0):
    np.random.seed(seed)
    _w = jnp.asarray

    def _rec_inputs():
        import jax
        import jax.numpy as jnp
        _rk = jax.random.key(seed)
        x = 7.22e-05 + 1 * jax.random.normal(jax.random.fold_in(_rk, 1), (8, 128, 512), jnp.float32)
        _lenS = 128 - jax.random.randint(jax.random.fold_in(_rk, 7), (8,), 0, max(1, 128 // 4) + 1, jnp.int32)
        _lenS2 = 128 - jax.random.randint(jax.random.fold_in(_rk, 8), (8,), 0, max(1, 128 // 4) + 1, jnp.int32)
        _ctx_4096P = jax.random.normal(jax.random.fold_in(_rk, 11), (8, 16, 512), jnp.float32)
        _ctx_4096c = jax.random.dirichlet(jax.random.fold_in(_rk, 511), 0.3 * jnp.ones((16,), jnp.float32), (8, 128))
        _ctx_4096t = jnp.einsum('bsk,bkd->bsd', _ctx_4096c, _ctx_4096P)
        _ctx_4096t = _ctx_4096t * jax.lax.rsqrt(jnp.mean(jnp.square(_ctx_4096t)) + 1e-12) * 0.953939
        ctx_4096 = 4.13588e-05 + 0.999923 * (_ctx_4096t + 0.3 * jax.random.normal(jax.random.fold_in(_rk, 611), (8, 128, 512), jnp.float32))
        _validS = jnp.arange(128)[None, :] < _lenS[:, None]
        _validS2 = jnp.arange(128)[None, :] < _lenS2[:, None]
        _causal = jnp.tril(jnp.ones((128, 128), dtype=bool))
        mask_BxSxS2_bk0 = jnp.logical_not(jnp.broadcast_to(_validS2[:, None, :], (8, 128, 128)))
        return (x, ctx_4096, mask_BxSxS2_bk0)
    x, ctx_4096, mask_BxSxS2_bk0 = _rec_inputs()

    def _L0_xattn_setup():
        import jax, jax.numpy as jnp
        import numpy as np
        B, LQ, LK, D, H, DH = (2, 128, 128, 512, 32, 128)
        EPS = 1e-05

        def _rmsnorm(x, weight):
            var = jnp.mean(jnp.square(x), axis=-1, keepdims=True)
            return x * jax.lax.rsqrt(var + EPS) * weight
        key = jax.random.key(seed)
        ks = jax.random.split(key, 8)
        scale = 0.02
        return {'hidden_states': jax.random.normal(ks[0], (B, LQ, D), jnp.float32), 'key_value_states': jax.random.normal(ks[1], (B, LK, D), jnp.float32), 'attention_mask': jax.random.randint(ks[2], (B, LQ, LK), 0, 2) > 0, 'position_bias': jax.random.normal(ks[3], (H, LQ, LK), jnp.float32), 'ln_weight': jnp.ones((D,), jnp.float32), 'w_q': jax.random.normal(ks[4], (H * DH, D), jnp.float32) * scale, 'w_k': jax.random.normal(ks[5], (H * DH, D), jnp.float32) * scale, 'w_v': jax.random.normal(ks[6], (H * DH, D), jnp.float32) * scale, 'w_out': jax.random.normal(ks[7], (D, H * DH), jnp.float32) * scale}
    _L0_xattn_all = _L0_xattn_setup()
    _L0_xattn_in = {k: v for k, v in _L0_xattn_all.items() if k in ('position_bias', 'ln_weight', 'w_q', 'w_k', 'w_v', 'w_out')}
    del _L0_xattn_all

    def _L0_ffn_setup():
        import jax, jax.numpy as jnp
        import numpy as np

        @jax.custom_vjp
        def ste_sign(w):
            return jnp.sign(w)

        def _ste_fwd(w):
            return (jnp.sign(w), w)

        def _ste_bwd(w, g):
            mask = ((w > -1) & (w < 1)).astype(g.dtype)
            return (g * mask,)
        ste_sign.defvjp(_ste_fwd, _ste_bwd)
        key = jax.random.key(seed)
        k = jax.random.split(key, 6)
        B, S, H, O, E = (4, 256, 512, 512, 8)
        return {'x': jax.random.normal(k[0], (B, S, H), dtype=jnp.float32), 'weight': jax.random.normal(k[1], (O, H), dtype=jnp.float32) * 0.02, 'bias': jax.random.normal(k[2], (O,), dtype=jnp.float32) * 0.02, 'gate_w': jax.random.normal(k[3], (E, H), dtype=jnp.float32) * 0.02, 'in_channel_scale': jax.random.normal(k[4], (E, H), dtype=jnp.float32), 'out_channel_scale': jax.random.normal(k[5], (E, O), dtype=jnp.float32)}
    _L0_ffn_all = _L0_ffn_setup()
    _L0_ffn_in = {k: v for k, v in _L0_ffn_all.items() if k in ('weight', 'bias', 'gate_w', 'in_channel_scale', 'out_channel_scale')}
    del _L0_ffn_all
    return {'x': x, 'ctx_4096': ctx_4096, 'mask_BxSxS2_bk0': mask_BxSxS2_bk0, 'L0_xattn_position_bias': _L0_xattn_in['position_bias'], 'L0_xattn_ln_weight': _L0_xattn_in['ln_weight'], 'L0_xattn_w_q': _L0_xattn_in['w_q'], 'L0_xattn_w_k': _L0_xattn_in['w_k'], 'L0_xattn_w_v': _L0_xattn_in['w_v'], 'L0_xattn_w_out': _L0_xattn_in['w_out'], 'L0_ffn_weight': _L0_ffn_in['weight'], 'L0_ffn_bias': _L0_ffn_in['bias'], 'L0_ffn_gate_w': _L0_ffn_in['gate_w'], 'L0_ffn_in_channel_scale': _L0_ffn_in['in_channel_scale'], 'L0_ffn_out_channel_scale': _L0_ffn_in['out_channel_scale']}

def reference(x, ctx_4096, mask_BxSxS2_bk0, L0_xattn_position_bias, L0_xattn_ln_weight, L0_xattn_w_q, L0_xattn_w_k, L0_xattn_w_v, L0_xattn_w_out, L0_ffn_weight, L0_ffn_bias, L0_ffn_gate_w, L0_ffn_in_channel_scale, L0_ffn_out_channel_scale):
    import jax
    import jax.numpy as jnp

    def _L0_xattn_ref(hidden_states, key_value_states, attention_mask, position_bias, ln_weight, w_q, w_k, w_v, w_out):
        import jax, jax.numpy as jnp
        import numpy as np
        B, LQ, LK, D, H, DH = (2, 128, 128, 512, 32, 128)
        EPS = 1e-05

        def _rmsnorm(x, weight):
            var = jnp.mean(jnp.square(x), axis=-1, keepdims=True)
            return x * jax.lax.rsqrt(var + EPS) * weight
        x = _rmsnorm(hidden_states, ln_weight)
        b, lq, _ = x.shape
        lk = key_value_states.shape[1]
        h_q = (x @ w_q.T).reshape(b, lq, H, DH)
        h_k = (key_value_states @ w_k.T).reshape(b, lk, H, DH)
        h_v = (key_value_states @ w_v.T).reshape(b, lk, H, DH)
        score = jnp.einsum('bqhd,bkhd->bhqk', h_q, h_k)
        score = score + position_bias[None]
        m = attention_mask[:, None]
        score = jnp.where(m, score, -jnp.inf)
        score = jax.nn.softmax(score, axis=-1)
        score = jnp.where(m, score, 0.0)
        attn = jnp.einsum('bhqk,bkhd->bqhd', score, h_v).reshape(b, lq, H * DH)
        out = attn @ w_out.T
        return hidden_states + out

    def _L0_ffn_ref(x, weight, bias, gate_w, in_channel_scale, out_channel_scale):
        import jax, jax.numpy as jnp
        import numpy as np

        @jax.custom_vjp
        def ste_sign(w):
            return jnp.sign(w)

        def _ste_fwd(w):
            return (jnp.sign(w), w)

        def _ste_bwd(w, g):
            mask = ((w > -1) & (w < 1)).astype(g.dtype)
            return (g * mask,)
        ste_sign.defvjp(_ste_fwd, _ste_bwd)
        B, S, H = x.shape
        xf = x.reshape(-1, H)
        router_logits = xf @ gate_w.T
        routing = jax.nn.softmax(router_logits.astype(jnp.float32), axis=1).astype(x.dtype)
        in_scale = routing @ in_channel_scale
        out_scale = routing @ out_channel_scale
        wb = ste_sign(weight)
        out = xf * in_scale @ wb.T * out_scale + bias
        return out.reshape(B, S, -1)
    x = x + _L0_xattn_ref(_layernorm(x, axis=-1), ctx_4096, mask_BxSxS2_bk0, L0_xattn_position_bias, L0_xattn_ln_weight, L0_xattn_w_q, L0_xattn_w_k, L0_xattn_w_v, L0_xattn_w_out)
    x = x + _L0_ffn_ref(_layernorm(x, axis=-1), L0_ffn_weight, L0_ffn_bias, L0_ffn_gate_w, L0_ffn_in_channel_scale, L0_ffn_out_channel_scale)
    return x

_drawn_inputs = setup_inputs


def setup_inputs(seed=0):
    import zlib

    import numpy as np

    out = dict(_drawn_inputs(seed))
    spreads = {'L0_xattn_ln_weight': (1.0, 0.2)}
    factors = {'L0_ffn_bias': 8.0}
    for name, (base, spread) in spreads.items():
        noise = np.random.default_rng([zlib.crc32(name.encode()), seed]).standard_normal(out[name].shape)
        drawn = base * np.exp(spread * noise) if base else spread * noise
        out[name] = jnp.asarray(drawn.astype(out[name].dtype))
    for name, factor in factors.items():
        out[name] = (out[name] * factor).astype(out[name].dtype)
    return out
```

```python
from contextlib import ExitStack

import concourse.bass as bass
from concourse import mybir

F32 = mybir.dt.float32
F32R = mybir.dt.float32r
BF16 = mybir.dt.bfloat16
ALU = mybir.AluOpType
ACT = mybir.ActivationFunctionType
AX = mybir.AxisListType

P = 128
B = 8
D = 512
DC = D // P
NH = 32
HALF = B // 2
HT = HALF * P
VG = D // P
NG = NH // VG
NPAIR = NH // 2
E = 8
EPS = 1e-5
FFN_LAG = 3
MASKED = 2.0 ** 100


def pe_schedule():
    steps = [("K", 0, 0), ("K", 0, 1)]
    steps += [("V", 0, b) for b in range(6)] + [("X", i) for i in range(4)]
    steps += [("V", 0, 6), ("X", 4), ("X", 5), ("V", 0, 7), ("X", 6), ("X", 7), ("Q", 0, 0), ("Q", 0, 1)]
    for h in range(NH):
        group, j = divmod(h, VG)
        more, more_v = h + 1 < NH, group + 1 < NG
        if more:
            steps.append(("Q", h + 1, 0))
        steps.append(("S", h, 0))
        if more:
            steps.append(("Q", h + 1, 1))
        steps.append(("S", h, 1))
        if h % 2 == 0 and h:
            steps += [("OUT", h // 2 - 1, b) for b in range(HALF, B)]
        if more:
            steps += [("K", h + 1, 0), ("K", h + 1, 1)]
        steps.append(("T", h, 0))
        if more_v:
            steps.append(("V", group + 1, 2 * j))
        steps += [("PV", h, 0), ("T", h, 1)]
        if more_v:
            steps.append(("V", group + 1, 2 * j + 1))
        if more:
            steps.append(("PV", h, 1))
            if h % 2:
                steps += [("OUT", h // 2, b) for b in range(HALF)]
        else:
            steps += [("OUT", h // 2, b) for b in range(HALF)] + [("PV", h, 1)]
            steps += [("OUT", h // 2, b) for b in range(HALF, B)]
    return steps


def xattn_ffn(nc, x, ctx_t, mask, pos_bias, ln_w, wq, wk, wv, wo, ffn_w, ffn_bias, gate_t, in_scale, out_scale, out):
    steps = pe_schedule()
    proj_order = [s for s in steps if s[0] in "QKV"]
    nth_proj = {s: n for n, s in enumerate(proj_order)}
    out_order = [s for s in steps if s[0] == "OUT"]
    nth_out = {s[1:]: n for n, s in enumerate(out_order)}

    with ExitStack() as ctx:
        def sb(name, shape, dt):
            return ctx.enter_context(nc.sbuf_tensor(name, shape, dt))

        def bank(name):
            return ctx.enter_context(nc.psum_tensor(name, [P, 512], F32))

        def sem(name):
            return ctx.enter_context(nc.semaphore(name))

        x_hi, x_lo = sb("x_hi", [P, DC, B * P], F32R), sb("x_lo", [P, DC, B * P], F32R)
        c_hi, c_lo = sb("c_hi", [P, DC, B * P], F32R), sb("c_lo", [P, DC, B * P], F32R)
        wq_raw, wk_raw = sb("wq_raw", [P, DC, P], F32), sb("wk_raw", [P, DC, P], F32)
        wq_hi, wq_lo = sb("wq_hi", [P, DC, P], F32R), sb("wq_lo", [P, DC, P], F32R)
        wk_hi, wk_lo = sb("wk_hi", [P, DC, P], F32R), sb("wk_lo", [P, DC, P], F32R)
        wv_raw = sb("wv_raw", [P, DC, VG * P], F32)
        wv_hi, wv_lo = sb("wv_hi", [P, DC, VG * P], F32R), sb("wv_lo", [P, DC, VG * P], F32R)
        wo_raw = sb("wo_raw", [P, 2, D], F32)
        wo_hi, wo_lo = sb("wo_hi", [P, 2, D], F32R), sb("wo_lo", [P, 2, D], F32R)
        q_sb, k_sb = sb("q_sb", [P, 2, B * P], F32), sb("k_sb", [P, 2, B * P], F32)
        v_sb = sb("v_sb", [P, 2, B, VG * P], F32)
        bias_raw = sb("bias_raw", [P, P], F32)
        mask_neg = sb("mask_neg", [P, B, P], BF16)
        row_valid = sb("row_valid", [P, B], F32)
        bias_mask = sb("bias_mask", [P, 2, HALF, P], F32)
        probs = sb("probs", [P, 2, HALF, P], F32)
        probs_t = sb("probs_t", [P, 2, HALF * P], F32)
        neg_max, row_sum = sb("neg_max", [P, B], F32), sb("row_sum", [P, B], F32)
        inv_sum = sb("inv_sum", [P, B], F32)
        o_hi, o_lo = sb("o_hi", [P, 2, B * P], F32R), sb("o_lo", [P, 2, B * P], F32R)
        acc = sb("acc", [P, B, D], F32)
        ident = sb("ident", [P, P], F32)
        stats, mean_var = sb("stats", [P, B, 6], F32), sb("mean_var", [P, B, 2], F32)
        var_eps, std, rstd = sb("var_eps", [P, B], F32), sb("std", [P, B], F32), sb("rstd", [P, B], F32)
        ms, ms_eps = sb("ms", [P, B], F32), sb("ms_eps", [P, B], F32)
        rms, rrms = sb("rms", [P, B], F32), sb("rrms", [P, B], F32)
        logit_neg_max = sb("logit_neg_max", [P, B], F32)
        exps_sum, exps_inv = sb("exps_sum", [P, B], F32), sb("exps_inv", [P, B], F32)
        ctx_raw = v_sb[:, 1, :, :].rearrange("p (h c) t -> p h c t", h=2)
        hs_tiles = probs[:, :, :, :].rearrange("p r a b -> p r (a b)")
        h_tiles = probs_t
        lnw_bc = bias_mask[:, 1, :, :].rearrange("p a b -> p (a b)")
        mask_words = bias_mask[:, 0, 0:2, :].bitcast(mybir.dt.uint32)
        mask_u8 = bias_mask[:, 0, 0:2, :].bitcast(mybir.dt.uint8).rearrange("p a (b k) -> p (a b) k", k=P)
        ffn_neg = v_sb[:, 0, 0:4, :]
        ffn_bias_bc, in_scale_sb = v_sb[:, 0, 4, :], v_sb[0:E, 0, 5, :]
        out_scale_sb = v_sb[0:E, 0, 6, :]
        gate_sb = v_sb[:, 0, 7, 0:DC * E].rearrange("p (c e) -> p c e", c=DC)
        exps = v_sb[:, 0, 7, DC * E:DC * E + B * E].rearrange("p (t e) -> p t e", t=B)
        routing = v_sb[:, 0, 7, DC * E + B * E:DC * E + 2 * B * E].rearrange("p (t e) -> p t e", t=B)
        routing_t = wq_raw[0:E, 0:2, :]
        sign_w = wv_hi
        n_tiles, nt_tiles = hs_tiles, probs_t
        y_tiles = bias_mask[:, :, :, :].rearrange("p r a b -> p r (a b)")
        out_scale_tiles = q_sb[:, :, :].rearrange("p r (a n) -> p (r a) n", n=D)
        res_tiles = k_sb[:, :, :].rearrange("p r (a n) -> p (r a) n", n=D)

        proj_bank = [bank("proj0"), bank("proj1")]
        out_bank = [bank("out0"), bank("out1")]
        s_bank = [bank("s0"), bank("s1")]
        t_bank, o_bank = bank("t"), bank("o")

        d_wq, d_wk, d_wv, d_wo = sem("d_wq"), sem("d_wk"), sem("d_wv"), sem("d_wo")
        d_ctx = [sem("d_ctx0"), sem("d_ctx1")]
        d_x = [sem("d_x0"), sem("d_x1")]
        d_lnw, d_mask, d_bias = sem("d_lnw"), sem("d_mask"), sem("d_bias")
        d_ffn_w, d_ffn_small, d_out = sem("d_ffn_w"), sem("d_ffn_small"), sem("d_out")
        pe_proj, pe_out, pe_s, pe_t, pe_pv, pe_x = [sem(n) for n in ("pe_proj", "pe_out", "pe_s", "pe_t", "pe_pv", "pe_x")]
        pe_nt, pe_gate, pe_rt, pe_scale, pe_ffn = [sem(n) for n in ("pe_nt", "pe_gate", "pe_rt", "pe_scale", "pe_ffn")]
        a_proj, a_exp, a_pt, a_ohi = sem("a_proj"), sem("a_exp"), sem("a_pt"), sem("a_ohi")
        a_ctx_hi, a_x_hi, a_sqrt = sem("a_ctx_hi"), sem("a_x_hi"), sem("a_sqrt")
        a_wq_hi, a_wk_hi, a_wv_hi, a_wo_hi = sem("a_wq_hi"), sem("a_wk_hi"), sem("a_wv_hi"), sem("a_wo_hi")
        a_nt, a_rexp, a_rt, a_os, a_yhi = sem("a_nt"), sem("a_rexp"), sem("a_rt"), sem("a_os"), sem("a_yhi")
        v_score, v_max, v_probs = sem("v_score"), sem("v_max"), sem("v_probs")
        v_olo, v_acc, v_ctx_lo, v_x_lo = sem("v_olo"), sem("v_acc"), sem("v_ctx_lo"), sem("v_x_lo")
        v_mask, v_hs, v_h, v_chain = sem("v_mask"), sem("v_hs"), sem("v_h"), sem("v_chain")
        v_var, v_ms, v_sign = sem("v_var"), sem("v_ms"), sem("v_sign")
        v_fvar, v_n, v_rmax, v_routing = sem("v_fvar"), sem("v_n"), sem("v_rmax"), sem("v_routing")
        v_y, v_prod = sem("v_y"), sem("v_prod")
        g_zero, g_ident, g_bm = sem("g_zero"), sem("g_ident"), sem("g_bm")
        g_wq_lo, g_wk_lo, g_wv_lo, g_wo_lo = sem("g_wq_lo"), sem("g_wk_lo"), sem("g_wv_lo"), sem("g_wo_lo")
        g_acc, g_xb, g_ylo, g_res = sem("g_acc"), sem("g_xb"), sem("g_ylo"), sem("g_res")

        def half_no(h, half):
            return 2 * h + half

        def last_v(group):
            return nth_proj[("V", group, B - 1)] + 1

        ROOTS = {("ln", 0): 1, ("ln", 1): 2, ("rms", 0): 3, ("rms", 1): 4, ("ffn", 0): 5, ("ffn", 1): 6}
        block = ctx.enter_context(nc.Block())

        @block.sync
        def _(sp):
            sp.dma_start(wk_raw[:], wk[0]).then_inc(d_wk, 16)
            sp.dma_start(ctx_raw[:, 0], ctx_t[0]).then_inc(d_ctx[0], 16)
            sp.dma_start(ctx_raw[:, 1], ctx_t[1]).then_inc(d_ctx[1], 16)
            sp.dma_start(wv_raw[:], wv[0]).then_inc(d_wv, 16)
            for half in range(2):
                sp.dma_start(acc[:, half * HALF:(half + 1) * HALF, :],
                             x[half * HALF:(half + 1) * HALF].rearrange("b t n -> t b n")).then_inc(d_x[half], 16)
            sp.dma_start(lnw_bc, ln_w.rearrange("(a n) -> a n", a=1).to_broadcast([P, D])).then_inc(d_lnw, 16)
            sp.dma_start(wq_raw[:], wq[0]).then_inc(d_wq, 16)
            sp.dma_start(mask_words.rearrange("p a (b w) -> p (a b) w", b=B // 2), mask).then_inc(d_mask, 16)
            sp.dma_start(bias_raw[:], pos_bias[0]).then_inc(d_bias, 16)
            sp.dma_start(wo_raw[:], wo[0]).then_inc(d_wo, 16)

            def next_head(w, raw, arrived, lo_done, h):
                if h < NH:
                    sp.wait_ge(lo_done, h)
                    sp.dma_start(raw[:], w[h]).then_inc(arrived, 16)

            def next_values(group):
                if group < NG:
                    sp.wait_ge(g_wv_lo, group)
                    sp.dma_start(wv_raw[:], wv[group]).then_inc(d_wv, 16)

            next_head(wk, wk_raw, d_wk, g_wk_lo, 1)
            next_values(1)
            next_head(wq, wq_raw, d_wq, g_wq_lo, 1)
            next_head(wk, wk_raw, d_wk, g_wk_lo, 2)
            next_head(wq, wq_raw, d_wq, g_wq_lo, 2)
            sp.wait_ge(g_bm, half_no(0, 1) + 1)
            sp.dma_start(bias_raw[:], pos_bias[1]).then_inc(d_bias, 16)
            for h in range(NH):
                group, j = divmod(h, VG)
                if j == 0:
                    next_values(group + 2)
                if h + 2 < NH:
                    sp.wait_ge(g_bm, half_no(h + 1, 1) + 1)
                    sp.dma_start(bias_raw[:], pos_bias[h + 2]).then_inc(d_bias, 16)
                next_head(wq, wq_raw, d_wq, g_wq_lo, h + 3)
                pair = h // 2 + 1
                if h % 2 and pair < NPAIR:
                    sp.wait_ge(g_wo_lo, pair)
                    sp.dma_start(wo_raw[:], wo[pair]).then_inc(d_wo, 16)
                next_head(wk, wk_raw, d_wk, g_wk_lo, h + 3)
                if h == NH - VG:
                    sp.wait_ge(g_wv_lo, NG)
                    sp.dma_start(wv_raw[:], ffn_w).then_inc(d_ffn_w, 16)
                    sp.wait_ge(pe_pv, half_no(h - 1, 1) + 1)
                    sp.dma_start(ffn_bias_bc, ffn_bias.rearrange("(a n) -> a n", a=1).to_broadcast([P, D])).then_inc(d_ffn_small, 16)
                    sp.dma_start(in_scale_sb, in_scale).then_inc(d_ffn_small, 16)
                    sp.dma_start(out_scale_sb, out_scale).then_inc(d_ffn_small, 16)
                    sp.dma_start(gate_sb, gate_t).then_inc(d_ffn_small, 16)
            for i in range(B):
                sp.wait_ge(g_res, i + 1)
                sp.dma_start(out[i], acc[:, i, :]).then_inc(d_out, 16)
            sp.wait_ge(d_out, 16 * B)

        @block.gpsimd
        def _(pool):
            def low(lo, raw, hi, hi_done, count, done):
                pool.wait_ge(hi_done, count)
                pool.tensor_tensor(lo, raw, hi.bitcast(F32), ALU.subtract).then_inc(done, 1)

            def low_wq(h):
                if h < NH:
                    low(wq_lo[:], wq_raw[:], wq_hi[:], a_wq_hi, h + 1, g_wq_lo)

            def low_wk(h):
                if h < NH:
                    low(wk_lo[:], wk_raw[:], wk_hi[:], a_wk_hi, h + 1, g_wk_lo)

            def low_wv(group):
                low(wv_lo[:], wv_raw[:], wv_hi[:], a_wv_hi, group + 1, g_wv_lo)

            def bias_and_mask(h, half):
                pool.wait_ge(d_bias, 16 * (h + 1))
                if h == 0:
                    pool.wait_ge(v_mask, 2)
                    if half == 1:
                        pool.wait_ge(v_h, B)
                else:
                    pool.wait_ge(v_score, half_no(h - 1, half) + 1)
                pool.tensor_tensor(bias_mask[:, half], bias_raw[:, None, :].to_broadcast([P, HALF, P]),
                                   mask_neg[:, half * HALF:(half + 1) * HALF, :], ALU.add).then_inc(g_bm, 1)

            low_wk(0)
            pool.memset(ident[:], 0.0).then_inc(g_zero, 1)
            pool.wait_ge(g_zero, 1)
            pool.affine_select(out=ident[:], in_=ident[:], compare_op=ALU.not_equal, fill=1.0, base=0,
                               pattern=[[-1, P]], channel_multiplier=1).then_inc(g_ident, 1)
            low_wv(0)
            low_wq(0)
            low_wk(1)
            for i in range(B):
                pool.wait_ge(v_hs, i + 1)
                pool.tensor_tensor(acc[:, i, :], acc[:, i, :], hs_tiles[:, i % 2, :], ALU.add).then_inc(g_acc, 1)
            bias_and_mask(0, 0)
            bias_and_mask(0, 1)
            low_wq(1)
            for h in range(NH):
                group, j = divmod(h, VG)
                if j == 0 and group + 1 < NG:
                    low_wv(group + 1)
                if h + 1 < NH:
                    bias_and_mask(h + 1, 0)
                    bias_and_mask(h + 1, 1)
                low_wq(h + 2)
                if h % 2:
                    low(wo_lo[:], wo_raw[:], wo_hi[:], a_wo_hi, h // 2 + 1, g_wo_lo)
                low_wk(h + 2)
            pool.wait_ge(d_ffn_small, 64)
            for t in range(B + FFN_LAG):
                if t < B:
                    pool.wait_ge(v_n, t + 1)
                    pool.tensor_tensor(acc[:, t, :], acc[:, t, :], ffn_bias_bc, ALU.add).then_inc(g_xb, 1)
                i = t - FFN_LAG
                if 0 <= i < B:
                    pool.wait_ge(v_prod, i + 1)
                    pool.wait_ge(g_xb, i + 1)
                    pool.tensor_tensor(acc[:, i, :], acc[:, i, :], res_tiles[:, i % 4, :], ALU.add).then_inc(g_res, 1)
                i = t - 1
                if 0 <= i < B:
                    pool.wait_ge(a_yhi, i + 1)
                    pool.tensor_tensor(x_lo[:, :, i * P:(i + 1) * P], y_tiles[:, i % 2, :].rearrange("p (c t) -> p c t", c=DC),
                                       x_hi[:, :, i * P:(i + 1) * P].bitcast(F32), ALU.subtract).then_inc(g_ylo, 1)

        @block.scalar
        def _(act):
            def high(hi, raw, arrived, count, free, free_count, done):
                act.wait_ge(arrived, count)
                if free_count:
                    act.wait_ge(free, free_count)
                act.activation(hi, raw, ACT.Copy).then_inc(done, 1)

            def high_wq(h):
                if h < NH:
                    high(wq_hi[:], wq_raw[:], d_wq, 16 * (h + 1), pe_proj, h and nth_proj[("Q", h - 1, 1)] + 1, a_wq_hi)

            def high_wk(h):
                if h < NH:
                    high(wk_hi[:], wk_raw[:], d_wk, 16 * (h + 1), pe_proj, h and nth_proj[("K", h - 1, 1)] + 1, a_wk_hi)

            def high_wv(group):
                high(wv_hi[:], wv_raw[:], d_wv, 16 * (group + 1), pe_proj, group and last_v(group - 1), a_wv_hi)

            def evacuate(step):
                kind, n, part = step
                order = nth_proj[step]
                act.wait_ge(pe_proj, order + 1)
                if kind == "V":
                    to = v_sb[:, n % 2, part, :]
                else:
                    to = (q_sb if kind == "Q" else k_sb)[:, n % 2, part * HT:(part + 1) * HT]
                act.activation(to, proj_bank[order % 2][:], ACT.Copy).then_inc(a_proj, 1)

            def exponentials(h, half):
                act.wait_ge(v_max, half_no(h, half) + 1)
                for b in range(HALF):
                    col = half * HALF + b
                    last = act.activation(probs[:, half, b, :], probs[:, half, b, :], ACT.Exp,
                                          bias=neg_max[:, col:col + 1], accum_out=row_sum[:, col:col + 1])
                last.then_inc(a_exp, 1)

            def transposed(h, half):
                act.wait_ge(pe_t, half_no(h, half) + 1)
                if h:
                    act.wait_ge(pe_pv, half_no(h - 1, half) + 1)
                act.activation(probs_t[:, half, :], t_bank[:], ACT.Copy).then_inc(a_pt, 1)

            def out_high(h, half):
                act.wait_ge(pe_pv, half_no(h, half) + 1)
                if h >= 2:
                    act.wait_ge(pe_out, nth_out[(h // 2 - 1, half * HALF + HALF - 1)] + 1)
                act.activation(o_hi[:, h % 2, half * HT:(half + 1) * HT], o_bank[:], ACT.Copy).then_inc(a_ohi, 1)

            def root(to, frm, ready, count):
                act.wait_ge(ready, count)
                act.activation(to, frm, ACT.Sqrt).then_inc(a_sqrt, 1)

            def x_high(i):
                act.wait_ge(pe_x, i + 1)
                act.activation(x_hi[:, :, i * P:(i + 1) * P], s_bank[i % 2][:].rearrange("p (c t) -> p c t", c=DC),
                               ACT.Copy).then_inc(a_x_hi, 1)

            high_wk(0)
            for half in range(2):
                act.wait_ge(d_ctx[half], 16)
                for c in range(DC):
                    act.activation(c_hi[:, c, half * HT:(half + 1) * HT], ctx_raw[:, half, c, :], ACT.Copy).then_inc(a_ctx_hi, 1)
            high_wv(0)
            evacuate(("K", 0, 0))
            evacuate(("K", 0, 1))
            high_wq(0)
            high_wk(1)
            evacuate(("V", 0, 0))
            for n, (to, frm, ready) in enumerate([(std, var_eps, v_var), (rms, ms_eps, v_ms)]):
                for half in range(2):
                    tiles = slice(half * HALF, (half + 1) * HALF)
                    root(to[:, tiles], frm[:, tiles], ready, half + 1)
                    evacuate(("V", 0, 1 + 2 * n + half))
            evacuate(("V", 0, 5))
            for i in range(4):
                x_high(i)
            evacuate(("V", 0, 6))
            x_high(4)
            x_high(5)
            evacuate(("V", 0, 7))
            x_high(6)
            x_high(7)
            evacuate(("Q", 0, 0))
            evacuate(("Q", 0, 1))
            high_wq(1)
            for h in range(NH):
                group, j = divmod(h, VG)
                more, more_v = h + 1 < NH, group + 1 < NG
                if j == 0 and more_v:
                    high_wv(group + 1)
                if more:
                    evacuate(("Q", h + 1, 0))
                exponentials(h, 0)
                if more:
                    evacuate(("Q", h + 1, 1))
                exponentials(h, 1)
                high_wq(h + 2)
                if more:
                    evacuate(("K", h + 1, 0))
                if h % 2:
                    pair = h // 2
                    high(wo_hi[:], wo_raw[:], d_wo, 16 * (pair + 1), pe_out, pair and nth_out[(pair - 1, B - 1)] + 1, a_wo_hi)
                if more:
                    evacuate(("K", h + 1, 1))
                high_wk(h + 2)
                transposed(h, 0)
                if more_v:
                    evacuate(("V", group + 1, 2 * j))
                out_high(h, 0)
                transposed(h, 1)
                if more_v:
                    evacuate(("V", group + 1, 2 * j + 1))
                if more:
                    out_high(h, 1)
            out_high(NH - 1, 1)
            root(std[:, 0:HALF], var_eps[:, 0:HALF], v_fvar, 1)
            for t in range(B + 1):
                if t < B:
                    act.wait_ge(pe_nt, t + 1)
                    if t >= 2:
                        act.wait_ge(v_y, t - 1)
                    act.activation(nt_tiles[:, t % 2, :], t_bank[:], ACT.Copy).then_inc(a_nt, 1)
                    if t == 0:
                        root(std[:, HALF:B], var_eps[:, HALF:B], v_fvar, 2)
                    act.wait_ge(v_rmax, t + 1)
                    act.activation(exps[:, t, :], s_bank[0][:, 0:E], ACT.Exp, bias=logit_neg_max[:, t:t + 1],
                                   accum_out=exps_sum[:, t:t + 1]).then_inc(a_rexp, 1)
                i = t - 1
                if 0 <= i < B:
                    act.wait_ge(pe_rt, i + 1)
                    act.activation(routing_t[:, i % 2, :], s_bank[1][0:E, 0:P], ACT.Copy).then_inc(a_rt, 1)
                    act.wait_ge(v_y, i + 1)
                    act.activation(x_hi[:, :, i * P:(i + 1) * P], y_tiles[:, i % 2, :].rearrange("p (c t) -> p c t", c=DC),
                                   ACT.Copy).then_inc(a_yhi, 1)
                    act.wait_ge(pe_scale, 2 * i + 2)
                    if i >= 4:
                        act.wait_ge(v_prod, i - 3)
                    act.activation(out_scale_tiles[:, i % 4, :], out_bank[0][:], ACT.Copy).then_inc(a_os, 1)

        @block.vector
        def _(dve):
            chain = [0]

            def link(instruction):
                chain[0] += 1
                instruction.then_inc(v_chain, 1)
                dve.wait_ge(v_chain, chain[0])

            def scores(h, half):
                n = half_no(h, half)
                dve.wait_ge(pe_s, n + 1)
                dve.wait_ge(g_bm, n + 1)
                if h:
                    dve.wait_ge(pe_t, n - 1)
                dve.tensor_tensor(probs[:, half], s_bank[half][:].rearrange("p (b k) -> p b k", b=HALF),
                                  bias_mask[:, half], ALU.add).then_inc(v_score, 1)
                dve.wait_ge(v_score, n + 1)
                dve.tensor_reduce(neg_max[:, half * HALF:(half + 1) * HALF], probs[:, half], axis=AX.X, op=ALU.max,
                                  negate=True).then_inc(v_max, 1)

            def normalise(h, half):
                cols = slice(half * HALF, (half + 1) * HALF)
                dve.wait_ge(a_exp, half_no(h, half) + 1)
                link(dve.reciprocal(inv_sum[:, cols], row_sum[:, cols]))
                link(dve.tensor_tensor(inv_sum[:, cols], inv_sum[:, cols], row_valid[:, cols], ALU.mult))
                dve.tensor_tensor(probs[:, half], probs[:, half], inv_sum[:, cols, None].to_broadcast([P, HALF, P]),
                                  ALU.mult).then_inc(v_probs, 1)

            def out_low(h, half):
                dve.wait_ge(a_ohi, half_no(h, half) + 1)
                part = slice(half * HT, (half + 1) * HT)
                dve.tensor_tensor(o_lo[:, h % 2, part], o_bank[:], o_hi[:, h % 2, part].bitcast(F32),
                                  ALU.subtract).then_inc(v_olo, 1)

            def add_out(pair, b):
                n = nth_out[(pair, b)]
                dve.wait_ge(pe_out, n + 1)
                if pair:
                    dve.wait_ge(v_acc, nth_out[(pair - 1, b)] + 1)
                else:
                    dve.wait_ge(g_acc, b + 1)
                dve.tensor_tensor(acc[:, b, :], out_bank[n % 2][:], acc[:, b, :], ALU.add).then_inc(v_acc, 1)

            def x_low(i):
                dve.wait_ge(a_x_hi, i + 1)
                dve.tensor_tensor(x_lo[:, :, i * P:(i + 1) * P], s_bank[i % 2][:].rearrange("p (c t) -> p c t", c=DC),
                                  x_hi[:, :, i * P:(i + 1) * P].bitcast(F32), ALU.subtract).then_inc(v_x_lo, 1)

            def variances(half, ready):
                tiles = range(half * HALF, (half + 1) * HALF)
                for i in tiles:
                    last = dve.bn_aggr(mean_var[:, i, :], stats[:, i, :])
                link(last)
                dve.tensor_scalar(var_eps[:, tiles.start:tiles.stop], mean_var[:, tiles.start:tiles.stop, 1], EPS, None,
                                  ALU.add).then_inc(ready, 1)

            for half in range(2):
                for c in range(DC):
                    dve.wait_ge(a_ctx_hi, half * DC + c + 1)
                    dve.tensor_tensor(c_lo[:, c, half * HT:(half + 1) * HT], ctx_raw[:, half, c, :],
                                      c_hi[:, c, half * HT:(half + 1) * HT].bitcast(F32), ALU.subtract).then_inc(v_ctx_lo, 1)

            halves = [slice(0, HALF), slice(HALF, B)]
            for half in range(2):
                dve.wait_ge(d_x[half], 16)
                for i in range(half * HALF, (half + 1) * HALF):
                    last = dve.bn_stats(stats[:, i, :], acc[:, i, :])
                link(last)
                variances(half, v_var)
            for half, tiles in enumerate(halves):
                dve.wait_ge(a_sqrt, ROOTS["ln", half])
                link(dve.reciprocal(rstd[:, tiles], std[:, tiles]))
                link(dve.tensor_tensor(ms[:, tiles], mean_var[:, tiles, 1], rstd[:, tiles], ALU.mult))
                link(dve.tensor_tensor(ms[:, tiles], ms[:, tiles], rstd[:, tiles], ALU.mult))
                dve.tensor_scalar(ms_eps[:, tiles], ms[:, tiles], EPS, None, ALU.add).then_inc(v_ms, 1)
            for half, tiles in enumerate(halves):
                dve.wait_ge(a_sqrt, ROOTS["rms", half])
                link(dve.reciprocal(rrms[:, tiles], rms[:, tiles]))
            dve.wait_ge(d_lnw, 16)
            for i in range(B):
                if i >= 2:
                    dve.wait_ge(g_acc, i - 1)
                    dve.wait_ge(v_h, i - 1)
                dve.tensor_scalar(hs_tiles[:, i % 2, :], acc[:, i, :], mean_var[:, i, 0:1], rstd[:, i:i + 1],
                                  ALU.subtract, ALU.mult).then_inc(v_hs, 1)
                dve.wait_ge(v_hs, i + 1)
                if i >= 2:
                    dve.wait_ge(pe_x, i - 1)
                dve.scalar_tensor_tensor(out=h_tiles[:, i % 2, :], in0=hs_tiles[:, i % 2, :], scalar=rrms[:, i:i + 1],
                                         in1=lnw_bc, op0=ALU.mult, op1=ALU.mult).then_inc(v_h, 1)
                if i:
                    x_low(i - 1)
            x_low(B - 1)
            dve.wait_ge(d_mask, 16)
            dve.tensor_scalar(mask_neg[:], mask_u8[:], -1.0, MASKED, ALU.add, ALU.mult).then_inc(v_mask, 1)
            dve.tensor_reduce(row_valid[:], mask_u8[:], axis=AX.X, op=ALU.max).then_inc(v_mask, 1)
            dve.wait_ge(v_mask, 2)

            for h in range(NH):
                scores(h, 0)
                normalise(h, 0)
                scores(h, 1)
                even_pair = h // 2 - 1 if h % 2 == 0 and h else None
                if even_pair is not None:
                    add_out(even_pair, HALF)
                normalise(h, 1)
                if even_pair is not None:
                    for b in range(HALF + 1, B):
                        add_out(even_pair, b)
                out_low(h, 0)
                if h + 1 < NH:
                    out_low(h, 1)
                if h % 2:
                    for b in range(HALF):
                        add_out(h // 2, b)
                if h == NH - VG:
                    dve.wait_ge(d_ffn_w, 16)
                    dve.wait_ge(pe_pv, half_no(h - 1, 1) + 1)
                    dve.wait_ge(pe_proj, last_v(NG - 1))
                    link(dve.tensor_scalar(ffn_neg, wv_raw[:], 0.0, None, ALU.is_lt))
                    dve.scalar_tensor_tensor(out=sign_w[:], in0=wv_raw[:], scalar=0.0, in1=ffn_neg, op0=ALU.is_gt,
                                             op1=ALU.subtract).then_inc(v_sign, 1)

            out_low(NH - 1, 1)
            for b in range(HALF):
                dve.wait_ge(v_acc, nth_out[(NPAIR - 1, b)] + 1)
                last = dve.bn_stats(stats[:, b, :], acc[:, b, :])
                add_out(NPAIR - 1, HALF + b)
            link(last)
            variances(0, v_fvar)
            for b in range(HALF, B):
                dve.wait_ge(v_acc, nth_out[(NPAIR - 1, b)] + 1)
                last = dve.bn_stats(stats[:, b, :], acc[:, b, :])
            link(last)
            variances(1, v_fvar)

            def normal_tile(i):
                if i % HALF == 0:
                    tiles = slice(i, i + HALF)
                    dve.wait_ge(a_sqrt, ROOTS["ffn", i // HALF])
                    link(dve.reciprocal(rstd[:, tiles], std[:, tiles]))
                if i < 2:
                    dve.wait_ge(pe_t, 2 * NH)
                else:
                    dve.wait_ge(pe_nt, i - 1)
                dve.tensor_scalar(n_tiles[:, i % 2, :], acc[:, i, :], mean_var[:, i, 0:1], rstd[:, i:i + 1],
                                  ALU.subtract, ALU.mult).then_inc(v_n, 1)

            normal_tile(0)
            for t in range(B + FFN_LAG):
                if t + 1 < B:
                    normal_tile(t + 1)
                i = t - FFN_LAG
                if 0 <= i < B:
                    dve.wait_ge(pe_ffn, i + 1)
                    dve.wait_ge(a_os, i + 1)
                    if i >= 4:
                        dve.wait_ge(g_res, i - 3)
                    dve.tensor_tensor(res_tiles[:, i % 4, :], proj_bank[i % 2][:], out_scale_tiles[:, i % 4, :],
                                      ALU.mult).then_inc(v_prod, 1)
                if t < B:
                    dve.wait_ge(pe_gate, t + 1)
                    dve.tensor_reduce(logit_neg_max[:, t:t + 1], s_bank[0][:, 0:E], axis=AX.X, op=ALU.max,
                                      negate=True).then_inc(v_rmax, 1)
                    dve.wait_ge(a_rexp, t + 1)
                    link(dve.reciprocal(exps_inv[:, t:t + 1], exps_sum[:, t:t + 1]))
                    dve.tensor_scalar(routing[:, t, :], exps[:, t, :], exps_inv[:, t:t + 1], None, ALU.mult).then_inc(v_routing, 1)
                i = t - 1
                if 0 <= i < B:
                    dve.wait_ge(pe_scale, 2 * i + 1)
                    if i >= 2:
                        dve.wait_ge(g_ylo, i - 1)
                    dve.tensor_tensor(y_tiles[:, i % 2, :], o_bank[:], nt_tiles[:, i % 2, :], ALU.mult).then_inc(v_y, 1)

        @block.tensor
        def _(pe):
            def three(out_ap, pairs, done):
                for n, ((left_hi, left_lo), (right_hi, right_lo)) in enumerate(pairs):
                    pe.matmul(out_ap, left_hi, right_hi, start=n == 0, stop=False)
                    pe.matmul(out_ap, left_lo, right_hi, start=False, stop=False)
                    last = pe.matmul(out_ap, left_hi, right_lo, start=False, stop=n == len(pairs) - 1)
                last.then_inc(done, 1)

            def both(pair, *index):
                return pair[0][index], pair[1][index]

            everything = slice(None)

            def project(step):
                kind, n, part = step
                order = nth_proj[step]
                if order >= 2:
                    pe.wait_ge(a_proj, order - 1)
                if kind == "V":
                    pe.wait_ge(g_wv_lo, n + 1)
                    toks = slice(part * P, (part + 1) * P)
                    pairs = [(both((c_hi, c_lo), everything, c, toks), both((wv_hi, wv_lo), everything, c, everything))
                             for c in range(DC)]
                else:
                    w, a = ((wq_hi, wq_lo), (x_hi, x_lo)) if kind == "Q" else ((wk_hi, wk_lo), (c_hi, c_lo))
                    pe.wait_ge(g_wq_lo if kind == "Q" else g_wk_lo, n + 1)
                    toks = slice(part * HT, (part + 1) * HT)
                    pairs = [(both(w, everything, c, everything), both(a, everything, c, toks)) for c in range(DC)]
                    if kind == "Q" and n == 0:
                        pe.wait_ge(v_x_lo, HALF * (part + 1))
                if kind == "K" and n == 0:
                    for c in range(DC):
                        pe.wait_ge(v_ctx_lo, part * DC + c + 1)
                        (wh, wl), (ah, al) = pairs[c]
                        bank_ap = proj_bank[order % 2][:]
                        pe.matmul(bank_ap, wh, ah, start=c == 0, stop=False)
                        pe.matmul(bank_ap, wl, ah, start=False, stop=False)
                        last = pe.matmul(bank_ap, wh, al, start=False, stop=c == DC - 1)
                    last.then_inc(pe_proj, 1)
                else:
                    three(proj_bank[order % 2][:], pairs, pe_proj)

            def transpose_x(i):
                pe.wait_ge(v_h, i + 1)
                if i == 0:
                    pe.wait_ge(g_ident, 1)
                if i >= 2:
                    pe.wait_ge(v_x_lo, i - 1)
                for c in range(DC):
                    last = pe.transpose(s_bank[i % 2][:, c * P:(c + 1) * P], h_tiles[:, i % 2, c * P:(c + 1) * P], ident[:])
                last.then_inc(pe_x, 1)

            def score(h, half):
                n = half_no(h, half)
                pe.wait_ge(a_proj, max(nth_proj[("Q", h, half)], nth_proj[("K", h, half)]) + 1)
                if h:
                    pe.wait_ge(v_score, n - 1)
                else:
                    pe.wait_ge(v_x_lo, B)
                for b in range(HALF):
                    toks = slice(half * HT + b * P, half * HT + (b + 1) * P)
                    last = pe.matmul(s_bank[half][:, b * P:(b + 1) * P], q_sb[:, h % 2, toks], k_sb[:, h % 2, toks],
                                     start=True, stop=True)
                last.then_inc(pe_s, 1)

            def transpose_probs(h, half):
                n = half_no(h, half)
                pe.wait_ge(v_probs, n + 1)
                if n:
                    pe.wait_ge(a_pt, n)
                for b in range(HALF):
                    last = pe.transpose(t_bank[:, b * P:(b + 1) * P], probs[:, half, b, :], ident[:])
                last.then_inc(pe_t, 1)

            def probs_times_values(h, half):
                n = half_no(h, half)
                group, j = divmod(h, VG)
                pe.wait_ge(a_pt, n + 1)
                pe.wait_ge(a_proj, nth_proj[("V", group, half * HALF + HALF - 1)] + 1)
                if n:
                    pe.wait_ge(v_olo, n)
                for b in range(HALF):
                    last = pe.matmul(o_bank[:, b * P:(b + 1) * P], v_sb[:, group % 2, half * HALF + b, j * P:(j + 1) * P],
                                     probs_t[:, half, b * P:(b + 1) * P], start=True, stop=True)
                last.then_inc(pe_pv, 1)

            def output(pair, b):
                n = nth_out[(pair, b)]
                pe.wait_ge(g_wo_lo, pair + 1)
                pe.wait_ge(v_olo, half_no(2 * pair + 1, b // HALF) + 1 if b >= HALF else half_no(2 * pair + 1, 0) + 1)
                if n >= 2:
                    pe.wait_ge(v_acc, n - 1)
                toks = slice(b * P, (b + 1) * P)
                three(out_bank[n % 2][:], [(both((o_hi, o_lo), everything, k, toks), both((wo_hi, wo_lo), everything, k, everything))
                                           for k in range(2)], pe_out)

            run = {"X": transpose_x, "S": score, "T": transpose_probs, "PV": probs_times_values, "OUT": output}
            for step in steps:
                if step[0] in "QKV":
                    project(step)
                else:
                    run[step[0]](*step[1:])

            pe.wait_ge(d_ffn_small, 64)
            pe.wait_ge(v_sign, 1)
            for t in range(B + FFN_LAG):
                if t < B:
                    pe.wait_ge(v_n, t + 1)
                    pe.wait_ge(a_nt, t) if t else pe.wait_ge(a_pt, 2 * NH)
                    for c in range(DC):
                        last = pe.transpose(t_bank[:, c * P:(c + 1) * P], n_tiles[:, t % 2, c * P:(c + 1) * P], ident[:])
                    last.then_inc(pe_nt, 1)
                i = t - FFN_LAG
                if 0 <= i < B:
                    pe.wait_ge(g_ylo, i + 1)
                    if i >= 2:
                        pe.wait_ge(v_prod, i - 1)
                    toks = slice(i * P, (i + 1) * P)
                    for c in range(DC):
                        pe.matmul(proj_bank[i % 2][:], x_hi[:, c, toks], sign_w[:, c, :], start=c == 0, stop=False)
                        last = pe.matmul(proj_bank[i % 2][:], x_lo[:, c, toks], sign_w[:, c, :], start=False, stop=c == DC - 1)
                    last.then_inc(pe_ffn, 1)
                if t < B:
                    pe.wait_ge(a_nt, t + 1)
                    if t:
                        pe.wait_ge(a_rexp, t)
                    for c in range(DC):
                        last = pe.matmul(s_bank[0][:, 0:E], nt_tiles[:, t % 2, c * P:(c + 1) * P], gate_sb[:, c, :],
                                         start=c == 0, stop=c == DC - 1)
                    last.then_inc(pe_gate, 1)
                i = t - 1
                if 0 <= i < B:
                    pe.wait_ge(v_routing, i + 1)
                    if i:
                        pe.wait_ge(a_rt, i)
                    pe.transpose(s_bank[1][0:E, 0:P], routing[:, i, :], ident[:]).then_inc(pe_rt, 1)
                    pe.wait_ge(a_rt, i + 1)
                    pe.wait_ge(v_y, i) if i else pe.wait_ge(v_olo, 2 * NH)
                    for c in range(DC):
                        last = pe.matmul(o_bank[:, c * P:(c + 1) * P], in_scale_sb[:, c * P:(c + 1) * P],
                                         routing_t[:, i % 2, :], start=True, stop=True)
                    last.then_inc(pe_scale, 1)
                    pe.wait_ge(a_os, i) if i else pe.wait_ge(v_acc, len(out_order))
                    pe.matmul(out_bank[0][:], routing_t[:, i % 2, :], out_scale_sb, start=True, stop=True).then_inc(pe_scale, 1)


def kernel(**inputs):
    import numpy as np
    import concourse.bacc as bacc
    from concourse.bass_utils import run_bass_kernel_spmd

    a = {k: np.asarray(v) for k, v in inputs.items()}
    per_head = lambda w: w.reshape(NH, P, DC, P).transpose(0, 3, 2, 1)
    laid = {
        "x": a["x"],
        "ctx_t": a["ctx_4096"].reshape(2, HT, DC, P).transpose(0, 3, 2, 1),
        "mask": np.ascontiguousarray(a["mask_BxSxS2_bk0"].transpose(1, 0, 2)).view(np.uint32),
        "pos_bias": a["L0_xattn_position_bias"],
        "ln_w": a["L0_xattn_ln_weight"],
        "wq": per_head(a["L0_xattn_w_q"]),
        "wk": per_head(a["L0_xattn_w_k"]),
        "wv": a["L0_xattn_w_v"].reshape(NG, VG * P, DC, P).transpose(0, 3, 2, 1),
        "wo": a["L0_xattn_w_out"].reshape(D, NPAIR, 2, P).transpose(1, 3, 2, 0),
        "ffn_w": a["L0_ffn_weight"].reshape(D, DC, P).transpose(2, 1, 0),
        "ffn_bias": a["L0_ffn_bias"],
        "gate_t": a["L0_ffn_gate_w"].reshape(E, DC, P).transpose(2, 1, 0),
        "in_scale": a["L0_ffn_in_channel_scale"],
        "out_scale": a["L0_ffn_out_channel_scale"],
    }
    nc = bacc.Bacc("TRN2", target_bir_lowering=False, num_devices=1)
    arrays, args = {}, []
    for name, array in laid.items():
        arrays[f"in_{name}"] = np.ascontiguousarray(array)
        args.append(nc.dram_tensor(f"in_{name}", array.shape, mybir.dt.from_np(array.dtype), kind="ExternalInput").ap())
    args.append(nc.dram_tensor("out", (B, P, D), F32, kind="ExternalOutput").ap())
    xattn_ffn(nc, *args)
    return run_bass_kernel_spmd(nc, [arrays], core_ids=[0]).results[0]["out"]
```

```python
from contextlib import ExitStack

import concourse.bass as bass
from concourse import mybir

F32 = mybir.dt.float32
F32R = mybir.dt.float32r
BF16 = mybir.dt.bfloat16
ALU = mybir.AluOpType
ACT = mybir.ActivationFunctionType
AX = mybir.AxisListType

P = 128
B = 8
D = 512
DC = D // P
NH = 32
HALF = B // 2
HT = HALF * P
VG = D // P
NG = NH // VG
NPAIR = NH // 2
E = 8
EPS = 1e-5
MASKED = 2.0 ** 100


def schedule():
    steps = [("WK", 0), ("CTX", 0), ("CTX", 1), ("WV", 0), ("K", 0, 0), ("K", 0, 1), ("WQ", 0), ("WK", 1), ("V", 0, 0),
             ("LN",), ("V", 0, 1), ("H", 0), ("H", 1), ("V", 0, 2), ("X", 0), ("H", 2), ("V", 0, 3), ("X", 1), ("H", 3),
             ("V", 0, 4), ("X", 2), ("H", 4), ("V", 0, 5), ("X", 3), ("H", 5), ("V", 0, 6), ("X", 4), ("H", 6), ("X", 5),
             ("H", 7), ("V", 0, 7), ("MASK",), ("X", 6), ("X", 7), ("Q", 0, 0), ("Q", 0, 1), ("BM", 0, 0), ("BM", 0, 1),
             ("WQ", 1)]
    last = NH - 2
    for h in range(last):
        group, j = divmod(h, VG)
        if j == 0 and group + 1 < NG:
            steps.append(("WV", group + 1))
        outs = [("OUT", h // 2 - 1, b) for b in range(HALF, B)] if h % 2 == 0 and h else []
        if h + 1 < last:
            steps += [("Q", h + 1, 0), ("S", h, 0), ("BM", h + 1, 0), ("N", h, 0), ("Q", h + 1, 1), ("S", h, 1), ("WQ", h + 2),
                      ("K", h + 1, 0), *outs[:1], ("N", h, 1), *outs[1:2], ("BM", h + 1, 1)]
            if h % 2:
                steps.append(("WO", h // 2))
            if group + 1 < NG:
                steps += [*outs[2:], ("K", h + 1, 1), ("WK", h + 2), ("T", h, 0), ("V", group + 1, 2 * j), ("PV", h, 0),
                          ("T", h, 1), ("V", group + 1, 2 * j + 1), ("PV", h, 1)]
            else:
                steps += [("K", h + 1, 1), ("WK", h + 2), ("T", h, 0), outs[2], ("PV", h, 0), ("T", h, 1), outs[3], ("PV", h, 1)]
        else:
            steps += [("Q", last, 0), ("S", h, 0), ("BM", last, 0), ("N", h, 0), ("WQ", last + 1), ("K", last, 0), ("S", h, 1),
                      ("WK", last + 1), ("Q", last + 1, 0), ("N", h, 1), ("WO", h // 2), ("T", h, 0), ("K", last + 1, 0),
                      ("T", h, 1), ("PV", h, 0), ("Q", last + 1, 1), ("WQ", NH), ("PV", h, 1)]
        if h == NH - VG:
            steps.append(("SIGN",))
        if h % 2:
            steps += [("OUT", h // 2, b) for b in range(HALF)]
    a, b, pair = last, last + 1, last // 2
    steps += [("S", a, 0), ("BM", b, 0), ("S", b, 0), ("BM", b, 1), ("OUT", pair - 1, 4), ("N", a, 0), ("OUT", pair - 1, 5),
              ("N", b, 0), ("OUT", pair - 1, 6), ("T", a, 0), ("K", b, 1), ("WK", NH), ("PV", a, 0), ("T", b, 0),
              ("OUT", pair - 1, 7), ("WO", pair), ("BM", a, 1), ("PV", b, 0), ("Q", NH, 1)]
    for tile in range(HALF):
        steps += [("OUT", pair, tile), ("ST", tile)]
    steps += [("LN2", 0), ("S", b, 1), ("NT", 0), ("N", b, 1), ("NT", 1), ("K", NH, 1), ("S", a, 1), ("T", b, 1), ("TX", 0),
              ("PV", b, 1), ("G", 0), ("N", a, 1), ("TX", 1), ("RT", 0), ("G", 1), ("R", 0), ("NT", 2), ("T", a, 1), ("TX", 2),
              ("RT", 1), ("NT", 3), ("PV", a, 1), ("R", 1), ("M", 0), ("TX", 3), ("G", 2)]
    steps += [("OUT", pair, 4), ("ST", 4), ("RT", 2), ("OUT", pair, 5), ("ST", 5), ("R", 2), ("G", 3),
              ("OUT", pair, 6), ("ST", 6), ("RT", 3), ("OUT", pair, 7), ("ST", 7), ("LN2", 1), ("R", 3), ("NT", 4), ("M", 1),
              ("TX", 4), ("NT", 5), ("M", 2), ("TX", 5), ("G", 4), ("NT", 6), ("M", 3), ("RT", 4), ("G", 5), ("R", 4), ("TX", 6),
              ("NT", 7), ("RT", 5), ("M", 4), ("R", 5), ("TX", 7), ("G", 6), ("M", 5), ("RT", 6), ("G", 7), ("R", 6), ("RT", 7),
              ("M", 6), ("R", 7), ("M", 7)]
    return steps


def xattn_ffn(nc, x, ctx_t, mask, pos_bias, ln_w, wq, wk, wv, wo, ffn_w, ffn_bias, gate_t, in_scale, out_scale, out):
    steps = schedule()

    def count(*kinds):
        found = [step for step in steps if step[0] in kinds]
        assert len(set(found)) == len(found)
        return {step: n + 1 for n, step in enumerate(found)}

    nth_proj = count("Q", "K", "V")
    nth_att = {step[1:]: n for step, n in count("S").items()}
    nth_out = {step[1:]: n for step, n in count("OUT").items()}
    for kind in ("N", "T", "PV", "BM"):
        assert [step[1:] for step in count(kind)] == list(nth_att)

    def use(h, half):
        return NH if (h, half) == (NH - 2, 1) else h

    def head(u):
        return u if u < NH else NH - 2

    with ExitStack() as ctx:
        def sb(name, shape, dt):
            return ctx.enter_context(nc.sbuf_tensor(name, shape, dt))

        def bank(name):
            return ctx.enter_context(nc.psum_tensor(name, [P, 512], F32))

        def sem(name):
            return ctx.enter_context(nc.semaphore(name))

        x_hi, x_lo = sb("x_hi", [P, DC, B * P], F32R), sb("x_lo", [P, DC, B * P], F32R)
        c_hi, c_lo = sb("c_hi", [P, DC, B * P], F32R), sb("c_lo", [P, DC, B * P], F32R)
        wq_raw, wk_raw = sb("wq_raw", [P, DC, P], F32), sb("wk_raw", [P, DC, P], F32)
        wq_hi, wq_lo = sb("wq_hi", [P, DC, P], F32R), sb("wq_lo", [P, DC, P], F32R)
        wk_hi, wk_lo = sb("wk_hi", [P, DC, P], F32R), sb("wk_lo", [P, DC, P], F32R)
        wv_raw = sb("wv_raw", [P, DC, VG * P], F32)
        wv_hi, wv_lo = sb("wv_hi", [P, DC, VG * P], F32R), sb("wv_lo", [P, DC, VG * P], F32R)
        wo_raw = sb("wo_raw", [P, 2, D], F32)
        wo_hi, wo_lo = sb("wo_hi", [P, 2, D], F32R), sb("wo_lo", [P, 2, D], F32R)
        q_sb, k_sb = sb("q_sb", [P, 2, B * P], F32), sb("k_sb", [P, 2, B * P], F32)
        v_sb = sb("v_sb", [P, 2, B, VG * P], F32)
        bias_raw = sb("bias_raw", [P, P], F32)
        mask_neg = sb("mask_neg", [P, B, P], BF16)
        row_valid = sb("row_valid", [P, B], F32)
        bias_mask = sb("bias_mask", [P, 2, HALF, P], F32)
        probs = sb("probs", [P, 2, HALF, P], F32)
        probs_t = sb("probs_t", [P, 2, HALF * P], F32)
        neg_max, row_sum = sb("neg_max", [P, B], F32), sb("row_sum", [P, B], F32)
        inv_sum = sb("inv_sum", [P, B], F32)
        o_hi, o_lo = sb("o_hi", [P, 2, B * P], F32R), sb("o_lo", [P, 2, B * P], F32R)
        acc = sb("acc", [P, B, D], F32)
        ident = sb("ident", [P, P], F32)
        stats, mean_var = sb("stats", [P, B, 6], F32), sb("mean_var", [P, B, 2], F32)
        var_eps, std, rstd = sb("var_eps", [P, B], F32), sb("std", [P, B], F32), sb("rstd", [P, B], F32)
        ms, ms_eps = sb("ms", [P, B], F32), sb("ms_eps", [P, B], F32)
        rms, rrms = sb("rms", [P, B], F32), sb("rrms", [P, B], F32)
        logit_neg_max = sb("logit_neg_max", [P, B], F32)
        exps_sum, exps_inv = sb("exps_sum", [P, B], F32), sb("exps_inv", [P, B], F32)
        ctx_raw = v_sb[:, 1, :, :].rearrange("p (h c) t -> p h c t", h=2)
        hs_tiles = probs[:, :, :, :].rearrange("p r a b -> p r (a b)")
        h_tiles = probs_t
        lnw_bc = bias_mask[:, 1, :, :].rearrange("p a b -> p (a b)")
        mask_words = bias_mask[:, 0, 0:2, :].bitcast(mybir.dt.uint32)
        mask_u8 = bias_mask[:, 0, 0:2, :].bitcast(mybir.dt.uint8).rearrange("p a (b k) -> p (a b) k", k=P)
        ffn_neg = v_sb[:, 0, 0:4, :]
        n_tiles, nt_tiles = v_sb[:, 0, 0:2, :], v_sb[:, 0, 2:4, :]
        ffn_bias_bc, in_scale_sb = v_sb[:, 0, 4, :], v_sb[0:E, 0, 5, :]
        out_scale_sb = v_sb[0:E, 0, 6, :]
        gate_sb = v_sb[:, 0, 7, 0:DC * E].rearrange("p (c e) -> p c e", c=DC)
        exps = v_sb[:, 0, 7, DC * E:DC * E + B * E].rearrange("p (t e) -> p t e", t=B)
        routing = v_sb[:, 0, 7, DC * E + B * E:DC * E + 2 * B * E].rearrange("p (t e) -> p t e", t=B)
        routing_t = v_sb[0:E, 0, 7, DC * E + 2 * B * E:DC * E + 2 * B * E + 2 * P].rearrange("p (r t) -> p r t", r=2)
        y_tiles = [wq_raw, wk_raw]
        out_scale_tiles = wv_raw
        res_tiles = wo_raw
        sign_w = wv_hi

        proj_bank = [bank("proj0"), bank("proj1")]
        out_bank = [bank("out0"), bank("out1")]
        s_bank = [bank("s0"), bank("s1")]
        t_bank, o_bank = bank("t"), bank("o")

        d_wq, d_wk, d_wv, d_wo = sem("d_wq"), sem("d_wk"), sem("d_wv"), sem("d_wo")
        d_ctx = [sem("d_ctx0"), sem("d_ctx1")]
        d_x = [sem("d_x0"), sem("d_x1")]
        d_lnw, d_mask, d_bias = sem("d_lnw"), sem("d_mask"), sem("d_bias")
        d_ffn_w, d_ffn_small, d_out = sem("d_ffn_w"), sem("d_ffn_small"), sem("d_out")
        pe_proj, pe_out, pe_s, pe_t, pe_pv, pe_x = [sem(n) for n in ("pe_proj", "pe_out", "pe_s", "pe_t", "pe_pv", "pe_x")]
        pe_nt, pe_gate, pe_rt, pe_scale, pe_ffn = [sem(n) for n in ("pe_nt", "pe_gate", "pe_rt", "pe_scale", "pe_ffn")]
        a_proj, a_exp, a_pt, a_ohi = sem("a_proj"), sem("a_exp"), sem("a_pt"), sem("a_ohi")
        a_ctx_hi, a_x_hi, a_sqrt = sem("a_ctx_hi"), sem("a_x_hi"), sem("a_sqrt")
        a_wq_hi, a_wk_hi, a_wv_hi, a_wo_hi = sem("a_wq_hi"), sem("a_wk_hi"), sem("a_wv_hi"), sem("a_wo_hi")
        a_nt, a_rexp, a_rt, a_os, a_yhi = sem("a_nt"), sem("a_rexp"), sem("a_rt"), sem("a_os"), sem("a_yhi")
        v_score, v_max, v_probs = sem("v_score"), sem("v_max"), sem("v_probs")
        v_olo, v_acc, v_ctx_lo, v_x_lo = sem("v_olo"), sem("v_acc"), sem("v_ctx_lo"), sem("v_x_lo")
        v_mask, v_hs, v_h, v_chain = sem("v_mask"), sem("v_hs"), sem("v_h"), sem("v_chain")
        v_var, v_ms, v_sign = sem("v_var"), sem("v_ms"), sem("v_sign")
        v_fvar, v_n, v_rmax, v_routing = sem("v_fvar"), sem("v_n"), sem("v_rmax"), sem("v_routing")
        v_y, v_ylo, v_prod, v_stats = sem("v_y"), sem("v_ylo"), sem("v_prod"), sem("v_stats")
        g_zero, g_ident, g_bm = sem("g_zero"), sem("g_ident"), sem("g_bm")
        g_wq_lo, g_wk_lo, g_wv_lo, g_wo_lo = sem("g_wq_lo"), sem("g_wk_lo"), sem("g_wv_lo"), sem("g_wo_lo")
        g_acc, g_xb, g_res = sem("g_acc"), sem("g_xb"), sem("g_res")

        def last_proj(kind, n):
            return max(order for step, order in nth_proj.items() if step[:2] == (kind, n))

        def walk(parts):
            for step in steps:
                if step[0] in parts:
                    parts[step[0]](*step[1:])

        ROOTS = {("ln", 0): 1, ("ln", 1): 2, ("rms", 0): 3, ("rms", 1): 4, ("ffn", 0): 5, ("ffn", 1): 6}
        ATTENTIONS = len(nth_att)
        halves = [slice(0, HALF), slice(HALF, B)]

        def bias_load(n):
            return n // 2 if n < 2 * (NH - 2) else {0: NH - 2, 1: NH - 1, 2: NH - 1, 3: NH}[n - 2 * (NH - 2)]

        block = ctx.enter_context(nc.Block())

        @block.sync
        def _(sp):
            sp.dma_start(wk_raw[:], wk[0]).then_inc(d_wk, 16)
            sp.dma_start(ctx_raw[:, 0], ctx_t[0]).then_inc(d_ctx[0], 16)
            sp.dma_start(ctx_raw[:, 1], ctx_t[1]).then_inc(d_ctx[1], 16)
            sp.dma_start(wv_raw[:], wv[0]).then_inc(d_wv, 16)
            for half, tiles in enumerate(halves):
                sp.dma_start(acc[:, tiles, :], x[tiles].rearrange("b t n -> t b n")).then_inc(d_x[half], 16)
            sp.dma_start(lnw_bc, ln_w.rearrange("(a n) -> a n", a=1).to_broadcast([P, D])).then_inc(d_lnw, 16)
            sp.dma_start(wq_raw[:], wq[0]).then_inc(d_wq, 16)
            sp.dma_start(mask_words.rearrange("p a (b w) -> p (a b) w", b=B // 2), mask).then_inc(d_mask, 16)
            sp.dma_start(bias_raw[:], pos_bias[0]).then_inc(d_bias, 16)
            sp.dma_start(wo_raw[:], wo[0]).then_inc(d_wo, 16)

            def after_wq(u):
                if u < NH:
                    sp.wait_ge(g_wq_lo, u + 1)
                    sp.dma_start(wq_raw[:], wq[head(u + 1)]).then_inc(d_wq, 16)

            def after_wk(u):
                if u < NH:
                    sp.wait_ge(g_wk_lo, u + 1)
                    sp.dma_start(wk_raw[:], wk[head(u + 1)]).then_inc(d_wk, 16)

            def after_wo(pair):
                if pair + 1 < NPAIR:
                    sp.wait_ge(g_wo_lo, pair + 1)
                    sp.dma_start(wo_raw[:], wo[pair + 1]).then_inc(d_wo, 16)

            def after_wv(group):
                sp.wait_ge(g_wv_lo, group + 1)
                if group + 1 < NG:
                    sp.dma_start(wv_raw[:], wv[group + 1]).then_inc(d_wv, 16)
                else:
                    sp.dma_start(wv_raw[:], ffn_w).then_inc(d_ffn_w, 16)

            def after_bias(h, half):
                n = nth_att[h, half]
                if n < ATTENTIONS and bias_load(n) != bias_load(n - 1):
                    sp.wait_ge(g_bm, n)
                    sp.dma_start(bias_raw[:], pos_bias[head(bias_load(n))]).then_inc(d_bias, 16)

            def ffn_loads():
                sp.wait_ge(pe_pv, nth_att[NH - VG - 1, 1])
                sp.dma_start(ffn_bias_bc, ffn_bias.rearrange("(a n) -> a n", a=1).to_broadcast([P, D])).then_inc(d_ffn_small, 16)
                sp.dma_start(in_scale_sb, in_scale).then_inc(d_ffn_small, 16)
                sp.dma_start(out_scale_sb, out_scale).then_inc(d_ffn_small, 16)
                sp.dma_start(gate_sb, gate_t).then_inc(d_ffn_small, 16)

            def store(i):
                sp.wait_ge(g_res, i + 1)
                sp.dma_start(out[i], acc[:, i, :]).then_inc(d_out, 16)

            walk({"WQ": after_wq, "WK": after_wk, "WO": after_wo, "WV": after_wv, "BM": after_bias, "SIGN": ffn_loads, "M": store})
            sp.wait_ge(d_out, 16 * B)

        @block.gpsimd
        def _(pool):
            pool.memset(ident[:], 0.0).then_inc(g_zero, 1)
            pool.wait_ge(g_zero, 1)
            pool.affine_select(out=ident[:], in_=ident[:], compare_op=ALU.not_equal, fill=1.0, base=0,
                               pattern=[[-1, P]], channel_multiplier=1).then_inc(g_ident, 1)

            def low(lo, raw, hi, hi_done, done):
                def part(n):
                    pool.wait_ge(hi_done, n + 1)
                    pool.tensor_tensor(lo[:], raw[:], hi[:].bitcast(F32), ALU.subtract).then_inc(done, 1)
                return part

            def bias_and_mask(h, half):
                n = nth_att[h, half] - 1
                pool.wait_ge(d_bias, 16 * (bias_load(n) + 1))
                if n < 2:
                    pool.wait_ge(v_mask, 2)
                    pool.wait_ge(v_h, B)
                else:
                    pool.wait_ge(v_score, n - 1)
                pool.tensor_tensor(bias_mask[:, n % 2], bias_raw[:, None, :].to_broadcast([P, HALF, P]),
                                   mask_neg[:, halves[half], :], ALU.add).then_inc(g_bm, 1)

            def residual(i):
                pool.wait_ge(v_hs, i + 1)
                pool.tensor_tensor(acc[:, i, :], acc[:, i, :], hs_tiles[:, i % 2, :], ALU.add).then_inc(g_acc, 1)

            def ffn_bias_on(i):
                if i == 0:
                    pool.wait_ge(d_ffn_small, 64)
                pool.wait_ge(v_n, i + 1)
                pool.tensor_tensor(acc[:, i, :], acc[:, i, :], ffn_bias_bc, ALU.add).then_inc(g_xb, 1)

            def last_sum(i):
                pool.wait_ge(v_prod, i + 1)
                pool.wait_ge(g_xb, i + 1)
                pool.tensor_tensor(acc[:, i, :], acc[:, i, :], res_tiles[:, i % 2, :], ALU.add).then_inc(g_res, 1)

            walk({"WQ": low(wq_lo, wq_raw, wq_hi, a_wq_hi, g_wq_lo), "WK": low(wk_lo, wk_raw, wk_hi, a_wk_hi, g_wk_lo),
                  "WV": low(wv_lo, wv_raw, wv_hi, a_wv_hi, g_wv_lo), "WO": low(wo_lo, wo_raw, wo_hi, a_wo_hi, g_wo_lo),
                  "H": residual, "BM": bias_and_mask, "NT": ffn_bias_on, "M": last_sum})

        @block.scalar
        def _(act):
            def high(kind, hi, raw, arrived, done):
                def part(n):
                    act.wait_ge(arrived, 16 * (n + 1))
                    if n:
                        if kind == "O":
                            act.wait_ge(pe_out, nth_out[n - 1, B - 1])
                        else:
                            act.wait_ge(pe_proj, last_proj(kind, n - 1))
                    act.activation(hi[:], raw[:], ACT.Copy).then_inc(done, 1)
                return part

            def evacuate(kind):
                def part(n, which):
                    order = nth_proj[kind, n, which]
                    act.wait_ge(pe_proj, order)
                    if kind == "V":
                        to = v_sb[:, n % 2, which, :]
                    else:
                        to = (q_sb if kind == "Q" else k_sb)[:, head(n) % 2, which * HT:(which + 1) * HT]
                    act.activation(to, proj_bank[order % 2][:], ACT.Copy).then_inc(a_proj, 1)
                return part

            def context(half):
                act.wait_ge(d_ctx[half], 16)
                for c in range(DC):
                    act.activation(c_hi[:, c, half * HT:(half + 1) * HT], ctx_raw[:, half, c, :], ACT.Copy).then_inc(a_ctx_hi, 1)

            def exponentials(h, half):
                n = nth_att[h, half] - 1
                act.wait_ge(v_max, n + 1)
                for b in range(HALF):
                    col = n % 2 * HALF + b
                    last = act.activation(probs[:, n % 2, b, :], probs[:, n % 2, b, :], ACT.Exp,
                                          bias=neg_max[:, col:col + 1], accum_out=row_sum[:, col:col + 1])
                last.then_inc(a_exp, 1)

            def transposed(h, half):
                n = nth_att[h, half] - 1
                act.wait_ge(pe_t, n + 1)
                if n >= 2:
                    act.wait_ge(pe_pv, n - 1)
                act.activation(probs_t[:, n % 2, :], t_bank[:], ACT.Copy).then_inc(a_pt, 1)

            def out_high(h, half):
                act.wait_ge(pe_pv, nth_att[h, half])
                if h >= 2:
                    act.wait_ge(pe_out, nth_out[h // 2 - 1, half * HALF + HALF - 1])
                act.activation(o_hi[:, h % 2, half * HT:(half + 1) * HT], o_bank[:], ACT.Copy).then_inc(a_ohi, 1)

            def root(to, frm, half, ready):
                act.wait_ge(ready, half + 1)
                act.activation(to[:, halves[half]], frm[:, halves[half]], ACT.Sqrt).then_inc(a_sqrt, 1)

            def input_roots():
                for to, frm, ready in ((std, var_eps, v_var), (rms, ms_eps, v_ms)):
                    for half in range(2):
                        root(to, frm, half, ready)

            def x_high(i):
                act.wait_ge(pe_x, i + 1)
                act.activation(x_hi[:, :, i * P:(i + 1) * P], s_bank[i % 2][:].rearrange("p (c t) -> p c t", c=DC),
                               ACT.Copy).then_inc(a_x_hi, 1)

            def ffn_root(half):
                root(std, var_eps, half, v_fvar)

            def ffn_transposed(i):
                act.wait_ge(pe_nt, i + 1)
                if i >= 2:
                    act.wait_ge(v_y, i - 1)
                act.activation(nt_tiles[:, i % 2, :], s_bank[0][:], ACT.Copy).then_inc(a_nt, 1)

            def router_exponentials(i):
                act.wait_ge(v_rmax, i + 1)
                act.activation(exps[:, i, :], s_bank[1][:, 0:E], ACT.Exp, bias=logit_neg_max[:, i:i + 1],
                               accum_out=exps_sum[:, i:i + 1]).then_inc(a_rexp, 1)

            def routing_transposed(i):
                act.wait_ge(pe_rt, i + 1)
                if i >= 2:
                    act.wait_ge(pe_scale, 2 * i - 2)
                act.activation(routing_t[:, i % 2, :], t_bank[0:E, 0:P], ACT.Copy).then_inc(a_rt, 1)

            def scaled_high(i):
                act.wait_ge(v_y, i + 1)
                act.activation(x_hi[:, :, i * P:(i + 1) * P], y_tiles[i % 2][:], ACT.Copy).then_inc(a_yhi, 1)
                act.wait_ge(pe_scale, 2 * i + 2)
                if i >= 4:
                    act.wait_ge(v_prod, i - 3)
                act.activation(out_scale_tiles[:, i % 4, :], out_bank[0][:], ACT.Copy).then_inc(a_os, 1)

            walk({"WQ": high("Q", wq_hi, wq_raw, d_wq, a_wq_hi), "WK": high("K", wk_hi, wk_raw, d_wk, a_wk_hi),
                  "WV": high("V", wv_hi, wv_raw, d_wv, a_wv_hi), "WO": high("O", wo_hi, wo_raw, d_wo, a_wo_hi),
                  "Q": evacuate("Q"), "K": evacuate("K"), "V": evacuate("V"), "CTX": context, "LN": input_roots, "X": x_high,
                  "S": exponentials, "T": transposed, "PV": out_high, "LN2": ffn_root, "TX": ffn_transposed,
                  "G": router_exponentials, "RT": routing_transposed, "R": scaled_high})

        @block.vector
        def _(dve):
            chain = [0]

            def link(instruction):
                chain[0] += 1
                instruction.then_inc(v_chain, 1)
                dve.wait_ge(v_chain, chain[0])

            def context(half):
                for c in range(DC):
                    dve.wait_ge(a_ctx_hi, half * DC + c + 1)
                    dve.tensor_tensor(c_lo[:, c, half * HT:(half + 1) * HT], ctx_raw[:, half, c, :],
                                      c_hi[:, c, half * HT:(half + 1) * HT].bitcast(F32), ALU.subtract).then_inc(v_ctx_lo, 1)

            def variances(half, ready):
                for i in range(B)[halves[half]]:
                    last = dve.bn_aggr(mean_var[:, i, :], stats[:, i, :])
                link(last)
                dve.tensor_scalar(var_eps[:, halves[half]], mean_var[:, halves[half], 1], EPS, None, ALU.add).then_inc(ready, 1)

            def input_norms():
                for half in range(2):
                    dve.wait_ge(d_x[half], 16)
                    for i in range(B)[halves[half]]:
                        last = dve.bn_stats(stats[:, i, :], acc[:, i, :])
                    link(last)
                    variances(half, v_var)
                for half, tiles in enumerate(halves):
                    dve.wait_ge(a_sqrt, ROOTS["ln", half])
                    link(dve.reciprocal(rstd[:, tiles], std[:, tiles]))
                    link(dve.tensor_tensor(ms[:, tiles], mean_var[:, tiles, 1], rstd[:, tiles], ALU.mult))
                    link(dve.tensor_tensor(ms[:, tiles], ms[:, tiles], rstd[:, tiles], ALU.mult))
                    dve.tensor_scalar(ms_eps[:, tiles], ms[:, tiles], EPS, None, ALU.add).then_inc(v_ms, 1)
                for half, tiles in enumerate(halves):
                    dve.wait_ge(a_sqrt, ROOTS["rms", half])
                    link(dve.reciprocal(rrms[:, tiles], rms[:, tiles]))
                dve.wait_ge(d_lnw, 16)

            def normed(i):
                if i >= 2:
                    dve.wait_ge(g_acc, i - 1)
                    dve.wait_ge(v_h, i - 1)
                dve.tensor_scalar(hs_tiles[:, i % 2, :], acc[:, i, :], mean_var[:, i, 0:1], rstd[:, i:i + 1],
                                  ALU.subtract, ALU.mult).then_inc(v_hs, 1)
                dve.wait_ge(v_hs, i + 1)
                if i >= 2:
                    dve.wait_ge(pe_x, i - 1)
                dve.scalar_tensor_tensor(out=h_tiles[:, i % 2, :], in0=hs_tiles[:, i % 2, :], scalar=rrms[:, i:i + 1],
                                         in1=lnw_bc, op0=ALU.mult, op1=ALU.mult).then_inc(v_h, 1)

            def x_low(i):
                dve.wait_ge(a_x_hi, i + 1)
                dve.tensor_tensor(x_lo[:, :, i * P:(i + 1) * P], s_bank[i % 2][:].rearrange("p (c t) -> p c t", c=DC),
                                  x_hi[:, :, i * P:(i + 1) * P].bitcast(F32), ALU.subtract).then_inc(v_x_lo, 1)

            def masks():
                dve.wait_ge(d_mask, 16)
                dve.tensor_scalar(mask_neg[:], mask_u8[:], -1.0, MASKED, ALU.add, ALU.mult).then_inc(v_mask, 1)
                dve.tensor_reduce(row_valid[:], mask_u8[:], axis=AX.X, op=ALU.max).then_inc(v_mask, 1)
                dve.wait_ge(v_mask, 2)

            def scores(h, half):
                n = nth_att[h, half] - 1
                dve.wait_ge(pe_s, n + 1)
                dve.wait_ge(g_bm, n + 1)
                if n >= 2:
                    dve.wait_ge(pe_t, n - 1)
                dve.tensor_tensor(probs[:, n % 2], s_bank[n % 2][:].rearrange("p (b k) -> p b k", b=HALF),
                                  bias_mask[:, n % 2], ALU.add).then_inc(v_score, 1)
                dve.wait_ge(v_score, n + 1)
                dve.tensor_reduce(neg_max[:, halves[n % 2]], probs[:, n % 2], axis=AX.X, op=ALU.max, negate=True).then_inc(v_max, 1)

            def normalise(h, half):
                n = nth_att[h, half] - 1
                cols = halves[n % 2]
                dve.wait_ge(a_exp, n + 1)
                link(dve.reciprocal(inv_sum[:, cols], row_sum[:, cols]))
                link(dve.tensor_tensor(inv_sum[:, cols], inv_sum[:, cols], row_valid[:, halves[half]], ALU.mult))
                dve.tensor_tensor(probs[:, n % 2], probs[:, n % 2], inv_sum[:, cols, None].to_broadcast([P, HALF, P]),
                                  ALU.mult).then_inc(v_probs, 1)

            def out_low(h, half):
                dve.wait_ge(a_ohi, nth_att[h, half])
                part = slice(half * HT, (half + 1) * HT)
                dve.tensor_tensor(o_lo[:, h % 2, part], o_bank[:], o_hi[:, h % 2, part].bitcast(F32),
                                  ALU.subtract).then_inc(v_olo, 1)

            def add_out(pair, b):
                n = nth_out[pair, b]
                dve.wait_ge(pe_out, n)
                if pair:
                    dve.wait_ge(v_acc, nth_out[pair - 1, b])
                else:
                    dve.wait_ge(g_acc, b + 1)
                dve.tensor_tensor(acc[:, b, :], out_bank[n % 2][:], acc[:, b, :], ALU.add).then_inc(v_acc, 1)

            def signs():
                dve.wait_ge(d_ffn_w, 16)
                dve.wait_ge(pe_pv, nth_att[NH - VG - 1, 1])
                dve.wait_ge(pe_proj, last_proj("V", NG - 1))
                link(dve.tensor_scalar(ffn_neg, wv_raw[:], 0.0, None, ALU.is_lt))
                dve.scalar_tensor_tensor(out=sign_w[:], in0=wv_raw[:], scalar=0.0, in1=ffn_neg, op0=ALU.is_gt,
                                         op1=ALU.subtract).then_inc(v_sign, 1)

            def ffn_statistics(b):
                dve.wait_ge(v_acc, nth_out[NPAIR - 1, b])
                dve.bn_stats(stats[:, b, :], acc[:, b, :]).then_inc(v_stats, 1)

            def ffn_norms(half):
                dve.wait_ge(v_stats, (half + 1) * HALF)
                variances(half, v_fvar)

            def normal_tile(i):
                if i % HALF == 0:
                    tiles = halves[i // HALF]
                    dve.wait_ge(a_sqrt, ROOTS["ffn", i // HALF])
                    link(dve.reciprocal(rstd[:, tiles], std[:, tiles]))
                if i < 2:
                    dve.wait_ge(v_sign, 1)
                else:
                    dve.wait_ge(pe_nt, i - 1)
                dve.tensor_scalar(n_tiles[:, i % 2, :], acc[:, i, :], mean_var[:, i, 0:1], rstd[:, i:i + 1],
                                  ALU.subtract, ALU.mult).then_inc(v_n, 1)

            def route(i):
                dve.wait_ge(pe_gate, i + 1)
                dve.tensor_reduce(logit_neg_max[:, i:i + 1], s_bank[1][:, 0:E], axis=AX.X, op=ALU.max, negate=True).then_inc(v_rmax, 1)
                dve.wait_ge(a_rexp, i + 1)
                link(dve.reciprocal(exps_inv[:, i:i + 1], exps_sum[:, i:i + 1]))
                dve.tensor_scalar(routing[:, i, :], exps[:, i, :], exps_inv[:, i:i + 1], None, ALU.mult).then_inc(v_routing, 1)

            def scale_tile(i):
                dve.wait_ge(pe_scale, 2 * i + 1)
                if i < 2:
                    dve.wait_ge(g_wk_lo if i else g_wq_lo, NH + 1)
                else:
                    dve.wait_ge(v_ylo, i - 1)
                dve.tensor_tensor(y_tiles[i % 2][:], o_bank[:].rearrange("p (c t) -> p c t", c=DC),
                                  nt_tiles[:, i % 2, :].rearrange("p (c t) -> p c t", c=DC), ALU.mult).then_inc(v_y, 1)
                dve.wait_ge(a_yhi, i + 1)
                dve.tensor_tensor(x_lo[:, :, i * P:(i + 1) * P], y_tiles[i % 2][:], x_hi[:, :, i * P:(i + 1) * P].bitcast(F32),
                                  ALU.subtract).then_inc(v_ylo, 1)

            def scale_product(i):
                dve.wait_ge(pe_ffn, i + 1)
                dve.wait_ge(a_os, i + 1)
                if i < 2:
                    dve.wait_ge(g_wo_lo, NPAIR)
                else:
                    dve.wait_ge(g_res, i - 1)
                dve.tensor_tensor(res_tiles[:, i % 2, :], proj_bank[i % 2][:], out_scale_tiles[:, i % 4, :],
                                  ALU.mult).then_inc(v_prod, 1)

            walk({"CTX": context, "LN": input_norms, "H": normed, "X": x_low, "MASK": masks, "S": scores, "N": normalise,
                  "PV": out_low, "OUT": add_out, "SIGN": signs, "ST": ffn_statistics, "LN2": ffn_norms, "NT": normal_tile,
                  "G": route, "R": scale_tile, "M": scale_product})

        @block.tensor
        def _(pe):
            freed = {}

            def take(bank_tensor):
                if bank_tensor.name in freed:
                    pe.wait_ge(*freed[bank_tensor.name])
                return bank_tensor

            def read_by(bank_tensor, semaphore, value):
                freed[bank_tensor.name] = (semaphore, value)

            def both(pair, *index):
                return pair[0][index], pair[1][index]

            everything = slice(None)

            def three(bank_tensor, pairs, done, before=None):
                for n, ((left_hi, left_lo), (right_hi, right_lo)) in enumerate(pairs):
                    if before:
                        before(n)
                    pe.matmul(bank_tensor[:], left_hi, right_hi, start=n == 0, stop=False)
                    pe.matmul(bank_tensor[:], left_lo, right_hi, start=False, stop=False)
                    last = pe.matmul(bank_tensor[:], left_hi, right_lo, start=False, stop=n == len(pairs) - 1)
                last.then_inc(done, 1)

            def project(kind, w, acts, w_done):
                def part(n, which):
                    order = nth_proj[kind, n, which]
                    to = take(proj_bank[order % 2])
                    pe.wait_ge(w_done, n + 1)
                    before = None
                    if kind == "V":
                        toks = slice(which * P, (which + 1) * P)
                        if n == 0:
                            pe.wait_ge(v_ctx_lo, DC * (which // HALF + 1))
                        pairs = [(both(acts, everything, c, toks), both(w, everything, c, everything)) for c in range(DC)]
                    else:
                        toks = slice(which * HT, (which + 1) * HT)
                        if n == 0 and kind == "K":
                            before = lambda c: pe.wait_ge(v_ctx_lo, which * DC + c + 1)
                        if n == 0 and kind == "Q":
                            pe.wait_ge(v_x_lo, HALF * (which + 1))
                        pairs = [(both(w, everything, c, everything), both(acts, everything, c, toks)) for c in range(DC)]
                    three(to, pairs, pe_proj, before)
                    read_by(to, a_proj, order)
                return part

            def transpose_tile(to, tile, done):
                for c in range(DC):
                    last = pe.transpose(to[:, c * P:(c + 1) * P], tile[:, c * P:(c + 1) * P], ident[:])
                last.then_inc(done, 1)

            def transpose_x(i):
                pe.wait_ge(v_h, i + 1)
                if i == 0:
                    pe.wait_ge(g_ident, 1)
                transpose_tile(take(s_bank[i % 2]), h_tiles[:, i % 2, :], pe_x)
                read_by(s_bank[i % 2], v_x_lo, i + 1)

            def score(h, half):
                n = nth_att[h, half] - 1
                pe.wait_ge(a_proj, max(nth_proj[kind, use(h, half), half] for kind in "QK"))
                to = take(s_bank[n % 2])
                for b in range(HALF):
                    toks = slice(half * HT + b * P, half * HT + (b + 1) * P)
                    last = pe.matmul(to[:, b * P:(b + 1) * P], q_sb[:, h % 2, toks], k_sb[:, h % 2, toks], start=True, stop=True)
                last.then_inc(pe_s, 1)
                read_by(to, v_score, n + 1)

            def transpose_probs(h, half):
                n = nth_att[h, half] - 1
                pe.wait_ge(v_probs, n + 1)
                to = take(t_bank)
                for b in range(HALF):
                    last = pe.transpose(to[:, b * P:(b + 1) * P], probs[:, n % 2, b, :], ident[:])
                last.then_inc(pe_t, 1)
                read_by(to, a_pt, n + 1)

            def probs_times_values(h, half):
                n = nth_att[h, half] - 1
                group, j = divmod(h, VG)
                pe.wait_ge(a_pt, n + 1)
                pe.wait_ge(a_proj, nth_proj["V", group, half * HALF + HALF - 1])
                to = take(o_bank)
                for b in range(HALF):
                    last = pe.matmul(to[:, b * P:(b + 1) * P], v_sb[:, group % 2, half * HALF + b, j * P:(j + 1) * P],
                                     probs_t[:, n % 2, b * P:(b + 1) * P], start=True, stop=True)
                last.then_inc(pe_pv, 1)
                read_by(to, v_olo, n + 1)

            def output(pair, b):
                n = nth_out[pair, b]
                pe.wait_ge(g_wo_lo, pair + 1)
                pe.wait_ge(v_olo, max(nth_att[2 * pair + k, b // HALF] for k in range(2)))
                to = take(out_bank[n % 2])
                toks = slice(b * P, (b + 1) * P)
                three(to, [(both((o_hi, o_lo), everything, k, toks), both((wo_hi, wo_lo), everything, k, everything))
                           for k in range(2)], pe_out)
                read_by(to, v_acc, n)

            def ffn_transpose(i):
                pe.wait_ge(v_n, i + 1)
                transpose_tile(take(s_bank[0]), n_tiles[:, i % 2, :], pe_nt)
                read_by(s_bank[0], a_nt, i + 1)

            def router(i):
                if i == 0:
                    pe.wait_ge(d_ffn_small, 64)
                pe.wait_ge(a_nt, i + 1)
                to = take(s_bank[1])
                for c in range(DC):
                    last = pe.matmul(to[:, 0:E], nt_tiles[:, i % 2, c * P:(c + 1) * P], gate_sb[:, c, :],
                                     start=c == 0, stop=c == DC - 1)
                last.then_inc(pe_gate, 1)
                read_by(to, a_rexp, i + 1)

            def transpose_routing(i):
                pe.wait_ge(v_routing, i + 1)
                pe.transpose(take(t_bank)[0:E, 0:P], routing[:, i, :], ident[:]).then_inc(pe_rt, 1)
                read_by(t_bank, a_rt, i + 1)

            def routed_scales(i):
                pe.wait_ge(a_rt, i + 1)
                to = take(o_bank)
                for c in range(DC):
                    last = pe.matmul(to[:, c * P:(c + 1) * P], in_scale_sb[:, c * P:(c + 1) * P], routing_t[:, i % 2, :],
                                     start=True, stop=True)
                last.then_inc(pe_scale, 1)
                read_by(to, v_y, i + 1)
                to = take(out_bank[0])
                pe.matmul(to[:], routing_t[:, i % 2, :], out_scale_sb, start=True, stop=True).then_inc(pe_scale, 1)
                read_by(to, a_os, i + 1)

            def ffn_product(i):
                pe.wait_ge(v_ylo, i + 1)
                if i == 0:
                    pe.wait_ge(v_sign, 1)
                to = take(proj_bank[i % 2])
                toks = slice(i * P, (i + 1) * P)
                for c in range(DC):
                    pe.matmul(to[:], x_hi[:, c, toks], sign_w[:, c, :], start=c == 0, stop=False)
                    last = pe.matmul(to[:], x_lo[:, c, toks], sign_w[:, c, :], start=False, stop=c == DC - 1)
                last.then_inc(pe_ffn, 1)
                read_by(to, v_prod, i + 1)

            walk({"Q": project("Q", (wq_hi, wq_lo), (x_hi, x_lo), g_wq_lo), "K": project("K", (wk_hi, wk_lo), (c_hi, c_lo), g_wk_lo),
                  "V": project("V", (wv_hi, wv_lo), (c_hi, c_lo), g_wv_lo), "X": transpose_x, "S": score, "T": transpose_probs,
                  "PV": probs_times_values, "OUT": output, "TX": ffn_transpose, "G": router, "RT": transpose_routing,
                  "R": routed_scales, "M": ffn_product})


def kernel(**inputs):
    import numpy as np
    import concourse.bacc as bacc
    from concourse.bass_utils import run_bass_kernel_spmd

    a = {k: np.asarray(v) for k, v in inputs.items()}
    per_head = lambda w: w.reshape(NH, P, DC, P).transpose(0, 3, 2, 1)
    laid = {
        "x": a["x"],
        "ctx_t": a["ctx_4096"].reshape(2, HT, DC, P).transpose(0, 3, 2, 1),
        "mask": np.ascontiguousarray(a["mask_BxSxS2_bk0"].transpose(1, 0, 2)).view(np.uint32),
        "pos_bias": a["L0_xattn_position_bias"],
        "ln_w": a["L0_xattn_ln_weight"],
        "wq": per_head(a["L0_xattn_w_q"]),
        "wk": per_head(a["L0_xattn_w_k"]),
        "wv": a["L0_xattn_w_v"].reshape(NG, VG * P, DC, P).transpose(0, 3, 2, 1),
        "wo": a["L0_xattn_w_out"].reshape(D, NPAIR, 2, P).transpose(1, 3, 2, 0),
        "ffn_w": a["L0_ffn_weight"].reshape(D, DC, P).transpose(2, 1, 0),
        "ffn_bias": a["L0_ffn_bias"],
        "gate_t": a["L0_ffn_gate_w"].reshape(E, DC, P).transpose(2, 1, 0),
        "in_scale": a["L0_ffn_in_channel_scale"],
        "out_scale": a["L0_ffn_out_channel_scale"],
    }
    nc = bacc.Bacc("TRN2", target_bir_lowering=False, num_devices=1)
    arrays, args = {}, []
    for name, array in laid.items():
        arrays[f"in_{name}"] = np.ascontiguousarray(array)
        args.append(nc.dram_tensor(f"in_{name}", array.shape, mybir.dt.from_np(array.dtype), kind="ExternalInput").ap())
    args.append(nc.dram_tensor("out", (B, P, D), F32, kind="ExternalOutput").ap())
    xattn_ffn(nc, *args)
    return run_bass_kernel_spmd(nc, [arrays], core_ids=[0]).results[0]["out"]
```

```python
from contextlib import ExitStack

import concourse.bass as bass
from concourse import mybir

F32 = mybir.dt.float32
F32R = mybir.dt.float32r
BF16 = mybir.dt.bfloat16
ALU = mybir.AluOpType
ACT = mybir.ActivationFunctionType
AX = mybir.AxisListType

P = 128
B = 8
D = 512
DC = D // P
NH = 32
HALF = B // 2
HT = HALF * P
VG = D // P
NG = NH // VG
NPAIR = NH // 2
E = 8
EPS = 1e-5
STACK = 64
WARM_UP = 14
MASKED = 2.0 ** 100


def schedule():
    steps = [("WARM",), ("WK", 0), ("CTX", 0), ("CTX", 1), ("K", 0, 0), ("WV", 0), ("K", 0, 1), ("V", 0, 0), ("LN", 0), ("V", 0, 1),
             ("RMS", 0), ("WQ", 0), ("RMSR", 0), ("H", 0), ("H", 1), ("V", 0, 2), ("V", 0, 3), ("X", 0), ("V", 0, 4), ("LN", 1),
             ("H", 2), ("RMS", 1), ("X", 1), ("H", 3), ("RMSR", 1), ("V", 0, 5), ("WK", 1), ("X", 2), ("H", 4), ("V", 0, 6),
             ("X", 3), ("H", 5), ("V", 0, 7), ("H", 6), ("X", 4), ("X", 5), ("Q", 0, 0), ("H", 7), ("X", 6), ("X", 7), ("K", 1, 0),
             ("MASK",), ("Q", 0, 1), ("BM", 0, 0), ("BM", 0, 1), ("WQ", 1), ("K", 1, 1), ("WK", 2)]
    last = NH - 2
    for h in range(last):
        group, j = divmod(h, VG)
        outs = [("OUT", h // 2 - 1, b) for b in range(HALF, B)] if h % 2 == 0 and h else []
        signs = [("SIGN", c) for c in range(DC)] if h == NH - VG else []
        wv = [("WV", group + 1)] if j == 0 and group + 1 < NG else []
        wo = [("WO", h // 2)] if h % 2 else []
        if h == 0:
            steps += [*wv, ("S", 0, 0), ("EXP", 0, 0), ("BM", 1, 0), ("N", 0, 0), ("Q", 1, 0), ("S", 0, 1), ("EXP", 0, 1),
                      ("Q", 1, 1), ("N", 0, 1), ("BM", 1, 1), ("T", 0, 0), ("WQ", 2), ("V", 1, 0), ("PV", 0, 0), ("T", 0, 1),
                      ("V", 1, 1), ("PV", 0, 1)]
        elif h + 1 < last:
            steps += [*wv, ("Q", h + 1, 0), ("S", h, 0), ("EXP", h, 0), ("BM", h + 1, 0), ("N", h, 0), ("Q", h + 1, 1),
                      ("S", h, 1), ("EXP", h, 1), ("WQ", h + 2), ("K", h + 1, 0), *outs[:1], ("N", h, 1), *outs[1:2],
                      ("BM", h + 1, 1), *wo]
            if group + 1 < NG:
                steps += [*outs[2:], ("K", h + 1, 1), ("WK", h + 2), ("T", h, 0), ("V", group + 1, 2 * j), ("PV", h, 0),
                          ("T", h, 1), ("V", group + 1, 2 * j + 1), ("PV", h, 1)]
            else:
                steps += [*signs[:2], ("K", h + 1, 1), ("WK", h + 2), ("T", h, 0), outs[2], ("PV", h, 0), ("T", h, 1), outs[3],
                          ("PV", h, 1), *signs[2:]]
        else:
            steps += [("Q", last, 0), ("WQ", last + 1), ("S", h, 0), ("EXP", h, 0), ("BM", last, 0), ("N", h, 0),
                      ("K", last, 0), ("WK", last + 1), ("S", h, 1), ("EXP", h, 1), ("Q", last + 1, 0), ("N", h, 1), *wo,
                      ("T", h, 0), ("Q", last + 1, 1), ("WQ", NH), ("PV", h, 0), ("T", h, 1), ("K", last + 1, 0), ("SCALES",),
                      ("PV", h, 1)]
        if h % 2:
            steps += [("OUT", h // 2, b) for b in range(HALF)]
    a, b, pair = last, last + 1, last // 2
    steps += [("S", a, 0), ("EXP", a, 0), ("BM", b, 0), ("OUT", pair - 1, 4), ("K", b, 1), ("WK", NH), ("S", b, 0), ("EXP", b, 0),
              ("BM", b, 1), ("OUT", pair - 1, 5), ("N", a, 0), ("Q", NH, 1), ("OUT", pair - 1, 6), ("T", a, 0), ("N", b, 0),
              ("OUT", pair - 1, 7), ("PV", a, 0), ("BM", a, 1), ("T", b, 0), ("WO", pair), ("S", b, 1), ("PV", b, 0), ("EXP", b, 1),
              ("K", NH, 1), ("N", b, 1), ("OUT", pair, 0), ("S", a, 1), ("T", b, 1), ("EXP", a, 1), ("OUT", pair, 1),
              ("N", a, 1), ("PV", b, 1), ("OUT", pair, 2), ("ST", 0), ("T", a, 1), ("OUT", pair, 3), ("ST", 1), ("ST", 2), ("PV", a, 1),
              ("ST", 3), ("LN2", 0)]
    steps += [("NT", 0), ("NT", 1), ("OUT", pair, 4), ("ST", 4), ("TX", 0), ("TX", 1), ("NT", 2), ("NT", 3), ("OUT", pair, 5),
              ("G", 0), ("ST", 5), ("TX", 2), ("TX", 3), ("ROUTE", 0), ("OUT", pair, 6), ("RT", 0), ("RTC", 0), ("ST", 6), ("G", 1),
              ("R", 0), ("ROUTE", 1), ("RTC", 1), ("Y", 0), ("OUT", pair, 7), ("YL", 0), ("RT", 1), ("ST", 7), ("R", 1), ("OS", 0),
              ("LN2", 1), ("NT", 4), ("NT", 5), ("Y", 1), ("NT", 6), ("NT", 7), ("M", 0), ("OS", 1), ("M", 1), ("TX", 4), ("TX", 5),
              ("YL", 1), ("G", 2), ("ROUTE", 2), ("TX", 6), ("TX", 7), ("OS", 2), ("M", 2), ("RT", 2), ("RTC", 2), ("G", 3), ("R", 2),
              ("OS", 3), ("Y", 2), ("YL", 2), ("ROUTE", 3), ("M", 3), ("OS", 4), ("M", 4), ("RT", 3), ("RTC", 3), ("OS", 5), ("R", 3),
              ("Y", 3), ("YL", 3), ("M", 5), ("OS", 6), ("M", 6), ("OS", 7), ("M", 7)]
    return steps


def xattn_ffn(nc, x, ctx_t, mask, pos_bias, ln_w, wq, wk, wv, wo, ffn_w, ffn_bias, gate_t, scales, out):
    steps = schedule()

    def count(*kinds):
        found = [step for step in steps if step[0] in kinds]
        assert len(set(found)) == len(found)
        return {step: n + 1 for n, step in enumerate(found)}

    nth_proj = count("Q", "K", "V")
    nth_att = {step[1:]: n for step, n in count("S").items()}
    nth_out = {step[1:]: n for step, n in count("OUT").items()}
    for kind in ("EXP", "N", "T", "PV", "BM"):
        assert [step[1:] for step in count(kind)] == list(nth_att)

    def use(h, half):
        return NH if (h, half) == (NH - 2, 1) else h

    def head(u):
        return u if u < NH else NH - 2

    with ExitStack() as ctx:
        def sb(name, shape, dt):
            return ctx.enter_context(nc.sbuf_tensor(name, shape, dt))

        def bank(name):
            return ctx.enter_context(nc.psum_tensor(name, [P, 512], F32))

        def sem(name):
            return ctx.enter_context(nc.semaphore(name))

        x_hi, x_lo = sb("x_hi", [P, DC, B * P], F32R), sb("x_lo", [P, DC, B * P], F32R)
        c_hi, c_lo = sb("c_hi", [P, DC, B * P], F32R), sb("c_lo", [P, DC, B * P], F32R)
        wq_raw, wk_raw = sb("wq_raw", [P, DC, P], F32), sb("wk_raw", [P, DC, P], F32)
        wq_hi, wq_lo = sb("wq_hi", [P, DC, P], F32R), sb("wq_lo", [P, DC, P], F32R)
        wk_hi, wk_lo = sb("wk_hi", [P, DC, P], F32R), sb("wk_lo", [P, DC, P], F32R)
        wv_raw = sb("wv_raw", [P, DC, VG * P], F32)
        wv_hi, wv_lo = sb("wv_hi", [P, DC, VG * P], F32R), sb("wv_lo", [P, DC, VG * P], F32R)
        wo_raw = sb("wo_raw", [P, 2, D], F32)
        wo_hi, wo_lo = sb("wo_hi", [P, 2, D], F32R), sb("wo_lo", [P, 2, D], F32R)
        q_sb, k_sb = sb("q_sb", [P, 2, B * P], F32), sb("k_sb", [P, 2, B * P], F32)
        v_sb = sb("v_sb", [P, 2, B, VG * P], F32)
        bias_raw = sb("bias_raw", [P, P], F32)
        mask_neg = sb("mask_neg", [P, B, P], BF16)
        row_valid = sb("row_valid", [P, B], F32)
        bias_mask = sb("bias_mask", [P, 2, HALF, P], F32)
        probs = sb("probs", [P, 2, HALF, P], F32)
        probs_t = sb("probs_t", [P, 2, HALF * P], F32)
        neg_max, row_sum = sb("neg_max", [P, B], F32), sb("row_sum", [P, B], F32)
        inv_sum = sb("inv_sum", [P, B], F32)
        o_hi, o_lo = sb("o_hi", [P, 2, B * P], F32R), sb("o_lo", [P, 2, B * P], F32R)
        acc = sb("acc", [P, B, D], F32)
        ident = sb("ident", [P, P], F32)
        stats, mean_var = sb("stats", [P, B, 6], F32), sb("mean_var", [P, B, 2], F32)
        var_eps, std, rstd = sb("var_eps", [P, B], F32), sb("std", [P, B], F32), sb("rstd", [P, B], F32)
        ms, ms_eps = sb("ms", [P, B], F32), sb("ms_eps", [P, B], F32)
        rms, rrms = sb("rms", [P, B], F32), sb("rrms", [P, B], F32)
        logit_neg_max = sb("logit_neg_max", [P, B], F32)
        exps_sum, exps_inv = sb("exps_sum", [P, B], F32), sb("exps_inv", [P, B], F32)
        ctx_raw = v_sb[:, 1, :, :].rearrange("p (h c) t -> p h c t", h=2)
        hs_tiles = probs[:, :, :, :].rearrange("p r a b -> p r (a b)")
        h_tiles = probs_t
        lnw_bc = bias_mask[:, 1, :, :].rearrange("p a b -> p (a b)")
        mask_words = bias_mask[:, 0, 0:2, :].bitcast(mybir.dt.uint32)
        mask_u8 = bias_mask[:, 0, 0:2, :].bitcast(mybir.dt.uint8).rearrange("p a (b k) -> p (a b) k", k=P)
        ffn_neg = v_sb[:, 0, 0:4, :]
        n_tiles = v_sb[:, 0, 0:4, :]
        ffn_bias_bc = v_sb[:, 0, 4, :]
        scales_raw = v_sb[0:STACK, 0, 5:7, :]
        gate_sb = v_sb[:, 0, 7, 0:DC * E].rearrange("p (c e) -> p c e", c=DC)
        exps = v_sb[:, 0, 7, DC * E:DC * E + B * E].rearrange("p (t e) -> p t e", t=B)
        nt_tiles = k_sb[:].rearrange("p h (r n) -> p (h r) n", r=2)
        scales_split = wv_lo[0:STACK, 0:2, :]
        routing = wv_raw[:, 0, :].rearrange("p (t r) -> p t r", t=B)
        routing_t = c_hi[0:STACK, 0:2, 0:2 * P]
        y_tiles = [raw[:].rearrange("p c t -> p (c t)") for raw in (wq_raw, wk_raw)]
        out_scale_tiles = q_sb[:].rearrange("p h (r n) -> p (h r) n", r=2)
        res_tiles = wo_raw
        sign_w = wv_hi

        proj_bank = [bank("proj0"), bank("proj1")]
        out_bank = [bank("out0"), bank("out1")]
        s_bank = [bank("s0"), bank("s1")]
        t_bank, o_bank = bank("t"), bank("o")
        in_scale_bank = [o_bank, s_bank[1]]

        d_wq, d_wk, d_wv, d_wo = sem("d_wq"), sem("d_wk"), sem("d_wv"), sem("d_wo")
        d_ctx = [[sem(f"d_ctx{half}{c}") for c in range(DC)] for half in range(2)]
        d_first_wv = [sem(f"d_first_wv{c}") for c in range(DC)]
        d_x = [sem("d_x0"), sem("d_x1")]
        d_lnw, d_mask, d_bias = sem("d_lnw"), sem("d_mask"), sem("d_bias")
        d_ffn_w, d_ffn_small, d_out = sem("d_ffn_w"), sem("d_ffn_small"), sem("d_out")
        pe_proj, pe_out, pe_s, pe_t, pe_pv, pe_x = [sem(n) for n in ("pe_proj", "pe_out", "pe_s", "pe_t", "pe_pv", "pe_x")]
        pe_nt, pe_gate, pe_rt, pe_scale, pe_ffn = [sem(n) for n in ("pe_nt", "pe_gate", "pe_rt", "pe_scale", "pe_ffn")]
        pe_os, pe_warm = sem("pe_os"), sem("pe_warm")
        a_proj, a_exp, a_pt, a_ohi = sem("a_proj"), sem("a_exp"), sem("a_pt"), sem("a_ohi")
        a_ctx_hi, a_x_hi, a_sqrt = sem("a_ctx_hi"), sem("a_x_hi"), sem("a_sqrt")
        a_wq_hi, a_wk_hi, a_wv_hi, a_wo_hi = sem("a_wq_hi"), sem("a_wk_hi"), sem("a_wv_hi"), sem("a_wo_hi")
        a_nt, a_rexp, a_rt, a_os, a_yhi = sem("a_nt"), sem("a_rexp"), sem("a_rt"), sem("a_os"), sem("a_yhi")
        v_score, v_max, v_probs = sem("v_score"), sem("v_max"), sem("v_probs")
        v_olo, v_acc, v_ctx_lo, v_x_lo = sem("v_olo"), sem("v_acc"), sem("v_ctx_lo"), sem("v_x_lo")
        v_mask, v_hs, v_h, v_chain = sem("v_mask"), sem("v_hs"), sem("v_h"), sem("v_chain")
        v_var, v_ms, v_sign = sem("v_var"), sem("v_ms"), sem("v_sign")
        v_fvar, v_n, v_rmax, v_routing = sem("v_fvar"), sem("v_n"), sem("v_rmax"), sem("v_routing")
        v_y, v_ylo, v_prod, v_stats = sem("v_y"), sem("v_ylo"), sem("v_prod"), sem("v_stats")
        v_scales, v_last_res = sem("v_scales"), sem("v_last_res")
        v_first_wk_lo, a_first_wv_hi, v_first_wv_lo = sem("v_first_wk_lo"), sem("a_first_wv_hi"), sem("v_first_wv_lo")
        g_zero, g_ident, g_bm = sem("g_zero"), sem("g_ident"), sem("g_bm")
        g_wq_lo, g_wk_lo, g_wv_lo, g_wo_lo = sem("g_wq_lo"), sem("g_wk_lo"), sem("g_wv_lo"), sem("g_wo_lo")
        g_acc, g_xb, g_res, g_clear = sem("g_acc"), sem("g_xb"), sem("g_res"), sem("g_clear")

        def last_proj(kind, n):
            return max(order for step, order in nth_proj.items() if step[:2] == (kind, n))

        def low_done(kind, n):
            if n == 0 and kind == "K":
                return v_first_wk_lo, 1
            if n == 0 and kind == "V":
                return v_first_wv_lo, DC
            return {"Q": g_wq_lo, "K": g_wk_lo, "V": g_wv_lo}[kind], n + (kind == "Q")

        def walk(parts):
            for step in steps:
                if step[0] in parts:
                    parts[step[0]](*step[1:])

        ROOTS = {("ln", 0): 1, ("rms", 0): 2, ("ln", 1): 3, ("rms", 1): 4, ("ffn", 0): 5, ("ffn", 1): 6}
        ATTENTIONS = len(nth_att)
        halves = [slice(0, HALF), slice(HALF, B)]

        def bias_load(n):
            return n // 2 if n < 2 * (NH - 2) else {0: NH - 2, 1: NH - 1, 2: NH - 1, 3: NH}[n - 2 * (NH - 2)]

        block = ctx.enter_context(nc.Block())

        @block.sync
        def _(sp):
            sp.dma_start(wk_raw[:], wk[0]).then_inc(d_wk, 16)
            for half in range(2):
                for c in range(DC):
                    sp.dma_start(ctx_raw[:, half, c, :], ctx_t[half, :, c, :]).then_inc(d_ctx[half][c], 16)
            for c in range(DC):
                sp.dma_start(wv_raw[:, c, :], wv[0, :, c, :]).then_inc(d_first_wv[c], 16)
            for half, tiles in enumerate(halves):
                sp.dma_start(acc[:, tiles, :], x[tiles].rearrange("b t n -> t b n")).then_inc(d_x[half], 16)
            sp.dma_start(lnw_bc, ln_w.rearrange("(a n) -> a n", a=1).to_broadcast([P, D])).then_inc(d_lnw, 16)
            sp.dma_start(wq_raw[:], wq[0]).then_inc(d_wq, 16)
            sp.dma_start(mask_words.rearrange("p a (b w) -> p (a b) w", b=B // 2), mask).then_inc(d_mask, 16)
            sp.dma_start(bias_raw[:], pos_bias[0]).then_inc(d_bias, 16)
            sp.dma_start(wo_raw[:], wo[0]).then_inc(d_wo, 16)

            def after_wq(u):
                if u < NH:
                    sp.wait_ge(g_wq_lo, u + 1)
                    sp.dma_start(wq_raw[:], wq[head(u + 1)]).then_inc(d_wq, 16)

            def after_wk(u):
                if u < NH:
                    sp.wait_ge(*low_done("K", u))
                    sp.dma_start(wk_raw[:], wk[head(u + 1)]).then_inc(d_wk, 16)

            def after_wo(pair):
                if pair + 1 < NPAIR:
                    sp.wait_ge(g_wo_lo, pair + 1)
                    sp.dma_start(wo_raw[:], wo[pair + 1]).then_inc(d_wo, 16)

            def after_wv(group):
                sp.wait_ge(*low_done("V", group))
                if group + 1 < NG:
                    sp.dma_start(wv_raw[:], wv[group + 1]).then_inc(d_wv, 16)
                else:
                    sp.dma_start(wv_raw[:], ffn_w).then_inc(d_ffn_w, 16)

            def after_bias(h, half):
                n = nth_att[h, half]
                if n < ATTENTIONS and bias_load(n) != bias_load(n - 1):
                    sp.wait_ge(g_bm, n)
                    sp.dma_start(bias_raw[:], pos_bias[head(bias_load(n))]).then_inc(d_bias, 16)

            def ffn_loads(c):
                if c:
                    return
                sp.wait_ge(pe_pv, nth_att[NH - VG - 1, 1])
                sp.dma_start(ffn_bias_bc, ffn_bias.rearrange("(a n) -> a n", a=1).to_broadcast([P, D])).then_inc(d_ffn_small, 16)
                sp.wait_ge(g_clear, 1)
                for row in (0, E, 32):
                    sp.dma_start(scales_raw[row:row + E], scales).then_inc(d_ffn_small, 16)
                sp.dma_start(gate_sb, gate_t).then_inc(d_ffn_small, 16)

            def store(i):
                if i < B - 1:
                    sp.wait_ge(g_res, i + 1)
                else:
                    sp.wait_ge(v_last_res, 1)
                sp.dma_start(out[i], acc[:, i, :]).then_inc(d_out, 16)

            walk({"WQ": after_wq, "WK": after_wk, "WO": after_wo, "WV": after_wv, "BM": after_bias, "SIGN": ffn_loads, "M": store})
            sp.wait_ge(d_out, 16 * B)

        @block.gpsimd
        def _(pool):
            pool.memset(ident[:], 0.0).then_inc(g_zero, 1)
            pool.wait_ge(g_zero, 1)
            pool.affine_select(out=ident[:], in_=ident[:], compare_op=ALU.not_equal, fill=1.0, base=0,
                               pattern=[[-1, P]], channel_multiplier=1).then_inc(g_ident, 1)

            def low(lo, raw, hi, hi_done, done, first=0):
                def part(n):
                    if n < first:
                        return
                    pool.wait_ge(hi_done, n if lo is wv_lo else n + 1)
                    pool.tensor_tensor(lo[:], raw[:], hi[:].bitcast(F32), ALU.subtract).then_inc(done, 1)
                return part

            def bias_and_mask(h, half):
                n = nth_att[h, half] - 1
                pool.wait_ge(d_bias, 16 * (bias_load(n) + 1))
                if n < 2:
                    pool.wait_ge(v_mask, 2)
                    pool.wait_ge(v_h, B)
                else:
                    pool.wait_ge(v_score, n - 1)
                pool.tensor_tensor(bias_mask[:, n % 2], bias_raw[:, None, :].to_broadcast([P, HALF, P]),
                                   mask_neg[:, halves[half], :], ALU.add).then_inc(g_bm, 1)

            def residual(i):
                pool.wait_ge(v_hs, i + 1)
                pool.tensor_tensor(acc[:, i, :], acc[:, i, :], hs_tiles[:, i % 2, :], ALU.add).then_inc(g_acc, 1)

            def ffn_bias_on(i):
                if i == 0:
                    pool.wait_ge(d_ffn_small, 80)
                pool.wait_ge(v_n, i + 1)
                pool.tensor_tensor(acc[:, i, :], acc[:, i, :], ffn_bias_bc, ALU.add).then_inc(g_xb, 1)

            def last_sum(i):
                if i == B - 1:
                    return
                pool.wait_ge(v_prod, i + 1)
                pool.wait_ge(g_xb, i + 1)
                pool.tensor_tensor(acc[:, i, :], acc[:, i, :], res_tiles[:, i % 2, :], ALU.add).then_inc(g_res, 1)

            def clear_scales(c):
                if c == 0:
                    pool.wait_ge(pe_pv, nth_att[NH - VG - 1, 1])
                    pool.memset(scales_raw, 0.0).then_inc(g_clear, 1)

            def clear_routing():
                pool.wait_ge(v_sign, DC)
                pool.memset(wv_raw[:, 0, :], 0.0).then_inc(g_clear, 1)

            walk({"SIGN": clear_scales, "SCALES": clear_routing, "WQ": low(wq_lo, wq_raw, wq_hi, a_wq_hi, g_wq_lo), "WK": low(wk_lo, wk_raw, wk_hi, a_wk_hi, g_wk_lo, 1),
                  "WV": low(wv_lo, wv_raw, wv_hi, a_wv_hi, g_wv_lo, 1), "WO": low(wo_lo, wo_raw, wo_hi, a_wo_hi, g_wo_lo),
                  "H": residual, "BM": bias_and_mask, "NT": ffn_bias_on, "M": last_sum})

        @block.scalar
        def _(act):
            def high(kind, hi, raw, arrived, done):
                def part(n):
                    if kind == "V" and n == 0:
                        for c in range(DC):
                            act.wait_ge(d_first_wv[c], 16)
                            act.activation(hi[:, c, :], raw[:, c, :], ACT.Copy).then_inc(a_first_wv_hi, 1)
                        return
                    act.wait_ge(arrived, 16 * (n if kind == "V" else n + 1))
                    if n:
                        if kind == "O":
                            act.wait_ge(pe_out, nth_out[n - 1, B - 1])
                        else:
                            act.wait_ge(pe_proj, last_proj(kind, n - 1))
                    act.activation(hi[:], raw[:], ACT.Copy).then_inc(done, 1)
                return part

            def evacuate(kind):
                def part(n, which):
                    order = nth_proj[kind, n, which]
                    act.wait_ge(pe_proj, order)
                    if kind == "V":
                        to = v_sb[:, n % 2, which, :]
                    else:
                        to = (q_sb if kind == "Q" else k_sb)[:, head(n) % 2, which * HT:(which + 1) * HT]
                    act.activation(to, proj_bank[order % 2][:], ACT.Copy).then_inc(a_proj, 1)
                return part

            def context(half):
                for c in range(DC):
                    act.wait_ge(d_ctx[half][c], 16)
                    act.activation(c_hi[:, c, half * HT:(half + 1) * HT], ctx_raw[:, half, c, :], ACT.Copy).then_inc(a_ctx_hi, 1)

            def exponentials(h, half):
                n = nth_att[h, half] - 1
                act.wait_ge(v_max, n + 1)
                for b in range(HALF):
                    col = n % 2 * HALF + b
                    last = act.activation(probs[:, n % 2, b, :], probs[:, n % 2, b, :], ACT.Exp,
                                          bias=neg_max[:, col:col + 1], accum_out=row_sum[:, col:col + 1])
                last.then_inc(a_exp, 1)

            def transposed(h, half):
                n = nth_att[h, half] - 1
                act.wait_ge(pe_t, n + 1)
                if n >= 2:
                    act.wait_ge(pe_pv, n - 1)
                act.activation(probs_t[:, n % 2, :], t_bank[:], ACT.Copy).then_inc(a_pt, 1)

            def out_high(h, half):
                act.wait_ge(pe_pv, nth_att[h, half])
                if h >= 2:
                    act.wait_ge(pe_out, nth_out[h // 2 - 1, half * HALF + HALF - 1])
                act.activation(o_hi[:, h % 2, half * HT:(half + 1) * HT], o_bank[:], ACT.Copy).then_inc(a_ohi, 1)

            def root(to, frm, half, ready):
                act.wait_ge(ready, half + 1)
                act.activation(to[:, halves[half]], frm[:, halves[half]], ACT.Sqrt).then_inc(a_sqrt, 1)

            def layer_roots(half):
                root(std, var_eps, half, v_var)

            def rms_roots(half):
                root(rms, ms_eps, half, v_ms)

            def x_high(i):
                act.wait_ge(pe_x, i + 1)
                act.activation(x_hi[:, :, i * P:(i + 1) * P], s_bank[i % 2][:].rearrange("p (c t) -> p c t", c=DC),
                               ACT.Copy).then_inc(a_x_hi, 1)

            def ffn_root(half):
                root(std, var_eps, half, v_fvar)

            def ffn_transposed(i):
                act.wait_ge(pe_nt, i + 1)
                if i >= 4:
                    act.wait_ge(v_y, 2 * (i // 2 - 1))
                act.activation(nt_tiles[:, i % 4, :], s_bank[i % 2][:], ACT.Copy).then_inc(a_nt, 1)

            def router_exponentials(p):
                act.wait_ge(v_rmax, p + 1)
                for i in (2 * p, 2 * p + 1):
                    last = act.activation(exps[:, i, :], t_bank[:, i % 2 * E:i % 2 * E + E], ACT.Exp,
                                          bias=logit_neg_max[:, i:i + 1], accum_out=exps_sum[:, i:i + 1])
                last.then_inc(a_rexp, 1)

            def routing_transposed(p):
                act.wait_ge(pe_rt, p + 1)
                if p >= 2:
                    act.wait_ge(pe_scale, 2 * (p - 1))
                    act.wait_ge(pe_os, 2 * (p - 1))
                act.activation(routing_t[:, p % 2, :], s_bank[0][0:STACK, 0:2 * P], ACT.Copy).then_inc(a_rt, 1)

            def scaled_high(p):
                toks = slice(2 * p * P, 2 * (p + 1) * P)
                for k in range(2):
                    act.wait_ge(v_y, 2 * p + k + 1)
                    act.activation(x_hi[:, 2 * k:2 * k + 2, toks], y_tiles[k].rearrange("p (c t) -> p c t", c=2),
                                   ACT.Copy).then_inc(a_yhi, 1)

            def out_scale(i):
                act.wait_ge(pe_os, i + 1)
                if i >= 4:
                    act.wait_ge(v_prod, i - 3)
                act.activation(out_scale_tiles[:, i % 4, :], out_bank[1][:], ACT.Copy).then_inc(a_os, 1)

            walk({"WQ": high("Q", wq_hi, wq_raw, d_wq, a_wq_hi), "WK": high("K", wk_hi, wk_raw, d_wk, a_wk_hi),
                  "WV": high("V", wv_hi, wv_raw, d_wv, a_wv_hi), "WO": high("O", wo_hi, wo_raw, d_wo, a_wo_hi),
                  "Q": evacuate("Q"), "K": evacuate("K"), "V": evacuate("V"), "CTX": context, "LN": layer_roots,
                  "RMS": rms_roots, "X": x_high,
                  "EXP": exponentials, "T": transposed, "PV": out_high, "LN2": ffn_root, "TX": ffn_transposed,
                  "G": router_exponentials, "RTC": routing_transposed, "YL": scaled_high, "OS": out_scale})

        @block.vector
        def _(dve):
            chain = [0]

            def link(instruction):
                chain[0] += 1
                instruction.then_inc(v_chain, 1)
                dve.wait_ge(v_chain, chain[0])

            def context(half):
                toks = slice(half * HT, (half + 1) * HT)
                for c in range(DC):
                    dve.wait_ge(a_ctx_hi, half * DC + c + 1)
                    dve.tensor_tensor(c_lo[:, c, toks], ctx_raw[:, half, c, :], c_hi[:, c, toks].bitcast(F32),
                                      ALU.subtract).then_inc(v_ctx_lo, 1)

            def first_wk_low(n):
                if n == 0:
                    dve.wait_ge(a_wk_hi, 1)
                    dve.tensor_tensor(wk_lo[:], wk_raw[:], wk_hi[:].bitcast(F32), ALU.subtract).then_inc(v_first_wk_lo, 1)

            def first_wv_low(n):
                if n == 0:
                    for c in range(DC):
                        dve.wait_ge(a_first_wv_hi, c + 1)
                        dve.tensor_tensor(wv_lo[:, c, :], wv_raw[:, c, :], wv_hi[:, c, :].bitcast(F32),
                                          ALU.subtract).then_inc(v_first_wv_lo, 1)

            def variances(half, ready):
                for i in range(B)[halves[half]]:
                    last = dve.bn_aggr(mean_var[:, i, :], stats[:, i, :])
                link(last)
                dve.tensor_scalar(var_eps[:, halves[half]], mean_var[:, halves[half], 1], EPS, None, ALU.add).then_inc(ready, 1)

            def input_statistics(half):
                dve.wait_ge(d_x[half], 16)
                for i in range(B)[halves[half]]:
                    last = dve.bn_stats(stats[:, i, :], acc[:, i, :])
                link(last)
                variances(half, v_var)

            def mean_squares(half):
                tiles = halves[half]
                dve.wait_ge(a_sqrt, ROOTS["ln", half])
                link(dve.reciprocal(rstd[:, tiles], std[:, tiles]))
                link(dve.tensor_tensor(ms[:, tiles], mean_var[:, tiles, 1], rstd[:, tiles], ALU.mult))
                link(dve.tensor_tensor(ms[:, tiles], ms[:, tiles], rstd[:, tiles], ALU.mult))
                dve.tensor_scalar(ms_eps[:, tiles], ms[:, tiles], EPS, None, ALU.add).then_inc(v_ms, 1)

            def rms_reciprocals(half):
                dve.wait_ge(a_sqrt, ROOTS["rms", half])
                link(dve.reciprocal(rrms[:, halves[half]], rms[:, halves[half]]))
                if half == 0:
                    dve.wait_ge(d_lnw, 16)

            def normed(i):
                if i >= 2:
                    dve.wait_ge(g_acc, i - 1)
                    dve.wait_ge(v_h, i - 1)
                dve.tensor_scalar(hs_tiles[:, i % 2, :], acc[:, i, :], mean_var[:, i, 0:1], rstd[:, i:i + 1],
                                  ALU.subtract, ALU.mult).then_inc(v_hs, 1)
                dve.wait_ge(v_hs, i + 1)
                if i >= 2:
                    dve.wait_ge(pe_x, i - 1)
                dve.scalar_tensor_tensor(out=h_tiles[:, i % 2, :], in0=hs_tiles[:, i % 2, :], scalar=rrms[:, i:i + 1],
                                         in1=lnw_bc, op0=ALU.mult, op1=ALU.mult).then_inc(v_h, 1)

            def x_low(i):
                dve.wait_ge(a_x_hi, i + 1)
                dve.tensor_tensor(x_lo[:, :, i * P:(i + 1) * P], s_bank[i % 2][:].rearrange("p (c t) -> p c t", c=DC),
                                  x_hi[:, :, i * P:(i + 1) * P].bitcast(F32), ALU.subtract).then_inc(v_x_lo, 1)

            def masks():
                dve.wait_ge(d_mask, 16)
                dve.tensor_scalar(mask_neg[:], mask_u8[:], -1.0, MASKED, ALU.add, ALU.mult).then_inc(v_mask, 1)
                dve.tensor_reduce(row_valid[:], mask_u8[:], axis=AX.X, op=ALU.max).then_inc(v_mask, 1)
                dve.wait_ge(v_mask, 2)

            def scores(h, half):
                n = nth_att[h, half] - 1
                dve.wait_ge(pe_s, n + 1)
                dve.wait_ge(g_bm, n + 1)
                if n >= 2:
                    dve.wait_ge(pe_t, n - 1)
                dve.tensor_tensor(probs[:, n % 2], s_bank[n % 2][:].rearrange("p (b k) -> p b k", b=HALF),
                                  bias_mask[:, n % 2], ALU.add).then_inc(v_score, 1)
                dve.wait_ge(v_score, n + 1)
                dve.tensor_reduce(neg_max[:, halves[n % 2]], probs[:, n % 2], axis=AX.X, op=ALU.max, negate=True).then_inc(v_max, 1)

            def normalise(h, half):
                n = nth_att[h, half] - 1
                cols = halves[n % 2]
                dve.wait_ge(a_exp, n + 1)
                link(dve.reciprocal(inv_sum[:, cols], row_sum[:, cols]))
                link(dve.tensor_tensor(inv_sum[:, cols], inv_sum[:, cols], row_valid[:, halves[half]], ALU.mult))
                dve.tensor_tensor(probs[:, n % 2], probs[:, n % 2], inv_sum[:, cols, None].to_broadcast([P, HALF, P]),
                                  ALU.mult).then_inc(v_probs, 1)

            def out_low(h, half):
                dve.wait_ge(a_ohi, nth_att[h, half])
                part = slice(half * HT, (half + 1) * HT)
                dve.tensor_tensor(o_lo[:, h % 2, part], o_bank[:], o_hi[:, h % 2, part].bitcast(F32),
                                  ALU.subtract).then_inc(v_olo, 1)

            def add_out(pair, b):
                n = nth_out[pair, b]
                dve.wait_ge(pe_out, n)
                if pair:
                    dve.wait_ge(v_acc, nth_out[pair - 1, b])
                else:
                    dve.wait_ge(g_acc, b + 1)
                dve.tensor_tensor(acc[:, b, :], out_bank[n % 2][:], acc[:, b, :], ALU.add).then_inc(v_acc, 1)

            def signs(c):
                dve.wait_ge(d_ffn_w, 16)
                dve.wait_ge(pe_pv, nth_att[NH - VG - 1, 1])
                dve.wait_ge(pe_proj, last_proj("V", NG - 1))
                link(dve.tensor_scalar(ffn_neg[:, c, :], wv_raw[:, c, :], 0.0, None, ALU.is_lt))
                dve.scalar_tensor_tensor(out=sign_w[:, c, :], in0=wv_raw[:, c, :], scalar=0.0, in1=ffn_neg[:, c, :],
                                         op0=ALU.is_gt, op1=ALU.subtract).then_inc(v_sign, 1)

            def ffn_statistics(b):
                dve.wait_ge(v_acc, nth_out[NPAIR - 1, b])
                dve.bn_stats(stats[:, b, :], acc[:, b, :]).then_inc(v_stats, 1)

            def ffn_norms(half):
                dve.wait_ge(v_stats, (half + 1) * HALF)
                variances(half, v_fvar)

            def normal_tile(i):
                if i % HALF == 0:
                    tiles = halves[i // HALF]
                    dve.wait_ge(a_sqrt, ROOTS["ffn", i // HALF])
                    link(dve.reciprocal(rstd[:, tiles], std[:, tiles]))
                if i < 4:
                    dve.wait_ge(v_sign, DC)
                else:
                    dve.wait_ge(pe_nt, i - 3)
                dve.tensor_scalar(n_tiles[:, i % 4, :], acc[:, i, :], mean_var[:, i, 0:1], rstd[:, i:i + 1],
                                  ALU.subtract, ALU.mult).then_inc(v_n, 1)

            def split_scales():
                dve.wait_ge(d_ffn_small, 80)
                link(dve.tensor_copy(scales_split, scales_raw))
                low = slice(32, 32 + E)
                dve.tensor_tensor(scales_split[low], scales_raw[low], scales_split[low].bitcast(F32),
                                  ALU.subtract).then_inc(v_scales, 1)

            def logit_maxima(p):
                pair = slice(2 * p, 2 * p + 2)
                dve.wait_ge(pe_gate, p + 1)
                dve.tensor_reduce(logit_neg_max[:, pair], t_bank[:, 0:2 * E].rearrange("p (t e) -> p t e", t=2), axis=AX.X,
                                  op=ALU.max, negate=True).then_inc(v_rmax, 1)

            def route(p):
                pair = slice(2 * p, 2 * p + 2)
                dve.wait_ge(a_rexp, p + 1)
                if p == 0:
                    dve.wait_ge(g_clear, 2)
                link(dve.reciprocal(exps_inv[:, pair], exps_sum[:, pair]))
                for i in (2 * p, 2 * p + 1):
                    high = routing[:, i, :].rearrange("p (a r) -> p a r", a=2)[:, :, 0:E]
                    last = dve.tensor_scalar(high.bitcast(F32R), exps[:, i, None, :].to_broadcast([P, 2, E]), exps_inv[:, i:i + 1],
                                             None, ALU.mult)
                link(last)
                for i in (2 * p, 2 * p + 1):
                    last = dve.scalar_tensor_tensor(out=routing[:, i, E:2 * E], in0=exps[:, i, :], scalar=exps_inv[:, i:i + 1],
                                                    in1=routing[:, i, 0:E], op0=ALU.mult, op1=ALU.subtract)
                last.then_inc(v_routing, 1)

            def scale_tiles(p):
                ring = slice(2 * p % 4, 2 * p % 4 + 2)
                for k in range(2):
                    dve.wait_ge(pe_scale, 2 * p + k + 1)
                    if p == 0:
                        dve.wait_ge(*low_done("K" if k else "Q", NH))
                    else:
                        dve.wait_ge(v_ylo, 2 * p - 1 + k)
                    nt_pair = nt_tiles[:, ring, :].rearrange("p r (c t) -> p c r t", c=DC)[:, 2 * k:2 * k + 2]
                    dve.tensor_tensor(y_tiles[k].rearrange("p (c r t) -> p c r t", c=2, r=2),
                                      in_scale_bank[k][:].rearrange("p (c r t) -> p c r t", c=2, r=2), nt_pair,
                                      ALU.mult).then_inc(v_y, 1)

            def scaled_low(p):
                toks = slice(2 * p * P, 2 * (p + 1) * P)
                for k in range(2):
                    chunks = slice(2 * k, 2 * k + 2)
                    dve.wait_ge(a_yhi, 2 * p + k + 1)
                    dve.tensor_tensor(x_lo[:, chunks, toks], y_tiles[k].rearrange("p (c t) -> p c t", c=2),
                                      x_hi[:, chunks, toks].bitcast(F32), ALU.subtract).then_inc(v_ylo, 1)

            def scale_product(i):
                dve.wait_ge(pe_ffn, i + 1)
                dve.wait_ge(a_os, i + 1)
                if i < 2:
                    dve.wait_ge(g_wo_lo, NPAIR)
                else:
                    dve.wait_ge(g_res, i - 1)
                dve.tensor_tensor(res_tiles[:, i % 2, :], proj_bank[i % 2][:], out_scale_tiles[:, i % 4, :],
                                  ALU.mult).then_inc(v_prod, 1)
                if i == B - 1:
                    dve.wait_ge(v_prod, B)
                    dve.wait_ge(g_xb, B)
                    dve.tensor_tensor(acc[:, i, :], acc[:, i, :], res_tiles[:, i % 2, :], ALU.add).then_inc(v_last_res, 1)

            walk({"WK": first_wk_low, "WV": first_wv_low,
                  "CTX": context, "LN": input_statistics, "RMS": mean_squares, "RMSR": rms_reciprocals, "H": normed,
                  "X": x_low, "MASK": masks, "S": scores, "N": normalise,
                  "PV": out_low, "OUT": add_out, "SIGN": signs, "ST": ffn_statistics, "LN2": ffn_norms, "NT": normal_tile,
                  "SCALES": split_scales, "G": logit_maxima, "ROUTE": route, "Y": scale_tiles, "YL": scaled_low, "M": scale_product})

        @block.tensor
        def _(pe):
            freed = {}

            def take(bank_tensor):
                if bank_tensor.name in freed:
                    pe.wait_ge(*freed[bank_tensor.name])
                return bank_tensor

            def read_by(bank_tensor, semaphore, value):
                freed[bank_tensor.name] = (semaphore, value)

            def both(pair, *index):
                return pair[0][index], pair[1][index]

            everything = slice(None)

            def three(bank_tensor, pairs, done, before=None):
                for n, ((left_hi, left_lo), (right_hi, right_lo)) in enumerate(pairs):
                    if before:
                        before("hi", n)
                    pe.matmul(bank_tensor[:], left_hi, right_hi, start=n == 0, stop=False)
                    if before:
                        before("left lo", n)
                    pe.matmul(bank_tensor[:], left_lo, right_hi, start=False, stop=False)
                    if before:
                        before("right lo", n)
                    last = pe.matmul(bank_tensor[:], left_hi, right_lo, start=False, stop=n == len(pairs) - 1)
                last.then_inc(done, 1)

            def first_keys(half):
                def before(what, c):
                    if what == "hi":
                        pe.wait_ge(a_wk_hi, 1)
                        pe.wait_ge(a_ctx_hi, half * DC + c + 1)
                    elif what == "left lo":
                        pe.wait_ge(*low_done("K", 0))
                    else:
                        pe.wait_ge(v_ctx_lo, half * DC + c + 1)
                return before

            def first_values(what, c):
                if what == "hi":
                    pe.wait_ge(a_first_wv_hi, c + 1)
                elif what == "right lo":
                    pe.wait_ge(v_first_wv_lo, c + 1)

            def project(kind, w, acts):
                def part(n, which):
                    order = nth_proj[kind, n, which]
                    to = take(proj_bank[order % 2])
                    before = None
                    if n == 0 and kind == "K":
                        before = first_keys(which)
                    elif n == 0 and kind == "V":
                        pe.wait_ge(v_ctx_lo, DC * (which // HALF + 1))
                        before = first_values
                    else:
                        pe.wait_ge(*low_done(kind, n))
                    if n == 0 and kind == "Q":
                        pe.wait_ge(v_x_lo, HALF * (which + 1))
                    if kind == "V":
                        toks = slice(which * P, (which + 1) * P)
                        pairs = [(both(acts, everything, c, toks), both(w, everything, c, everything)) for c in range(DC)]
                    else:
                        toks = slice(which * HT, (which + 1) * HT)
                        pairs = [(both(w, everything, c, everything), both(acts, everything, c, toks)) for c in range(DC)]
                    three(to, pairs, pe_proj, before)
                    read_by(to, a_proj, order)
                return part

            def warm_up():
                pe.wait_ge(g_ident, 1)
                for _ in range(WARM_UP):
                    last = pe.transpose(s_bank[0][:, 0:P], ident[:], ident[:])
                last.then_inc(pe_warm, 1)
                pe.wait_ge(pe_warm, 1)

            def transpose_tile(to, tile, done):
                for c in range(DC):
                    last = pe.transpose(to[:, c * P:(c + 1) * P], tile[:, c * P:(c + 1) * P], ident[:])
                last.then_inc(done, 1)

            def transpose_x(i):
                pe.wait_ge(v_h, i + 1)
                transpose_tile(take(s_bank[i % 2]), h_tiles[:, i % 2, :], pe_x)
                read_by(s_bank[i % 2], v_x_lo, i + 1)

            def score(h, half):
                n = nth_att[h, half] - 1
                pe.wait_ge(a_proj, max(nth_proj[kind, use(h, half), half] for kind in "QK"))
                to = take(s_bank[n % 2])
                for b in range(HALF):
                    toks = slice(half * HT + b * P, half * HT + (b + 1) * P)
                    last = pe.matmul(to[:, b * P:(b + 1) * P], q_sb[:, h % 2, toks], k_sb[:, h % 2, toks], start=True, stop=True)
                last.then_inc(pe_s, 1)
                read_by(to, v_score, n + 1)

            def transpose_probs(h, half):
                n = nth_att[h, half] - 1
                pe.wait_ge(v_probs, n + 1)
                to = take(t_bank)
                for b in range(HALF):
                    last = pe.transpose(to[:, b * P:(b + 1) * P], probs[:, n % 2, b, :], ident[:])
                last.then_inc(pe_t, 1)
                read_by(to, a_pt, n + 1)

            def probs_times_values(h, half):
                n = nth_att[h, half] - 1
                group, j = divmod(h, VG)
                pe.wait_ge(a_pt, n + 1)
                pe.wait_ge(a_proj, nth_proj["V", group, half * HALF + HALF - 1])
                to = take(o_bank)
                for b in range(HALF):
                    last = pe.matmul(to[:, b * P:(b + 1) * P], v_sb[:, group % 2, half * HALF + b, j * P:(j + 1) * P],
                                     probs_t[:, n % 2, b * P:(b + 1) * P], start=True, stop=True)
                last.then_inc(pe_pv, 1)
                read_by(to, v_olo, n + 1)

            def output(pair, b):
                n = nth_out[pair, b]
                pe.wait_ge(g_wo_lo, pair + 1)
                pe.wait_ge(v_olo, max(nth_att[2 * pair + k, b // HALF] for k in range(2)))
                to = take(out_bank[n % 2])
                toks = slice(b * P, (b + 1) * P)
                three(to, [(both((o_hi, o_lo), everything, k, toks), both((wo_hi, wo_lo), everything, k, everything))
                           for k in range(2)], pe_out)
                read_by(to, v_acc, n)

            def ffn_transpose(i):
                pe.wait_ge(v_n, i + 1)
                transpose_tile(take(s_bank[i % 2]), n_tiles[:, i % 4, :], pe_nt)
                read_by(s_bank[i % 2], a_nt, i + 1)

            def router(p):
                if p == 0:
                    pe.wait_ge(d_ffn_small, 80)
                to = take(t_bank)
                for i in (2 * p, 2 * p + 1):
                    pe.wait_ge(a_nt, i + 1)
                    for c in range(DC):
                        last = pe.matmul(to[:, i % 2 * E:i % 2 * E + E], nt_tiles[:, i % 4, c * P:(c + 1) * P], gate_sb[:, c, :],
                                         start=c == 0, stop=c == DC - 1)
                last.then_inc(pe_gate, 1)
                read_by(to, a_rexp, p + 1)

            def transpose_routing(p):
                pe.wait_ge(v_routing, p + 1)
                to = take(s_bank[0])
                for i in (2 * p, 2 * p + 1):
                    last = pe.transpose(to[0:STACK, i % 2 * P:(i % 2 + 1) * P], routing[:, i, :], ident[:])
                last.then_inc(pe_rt, 1)
                read_by(to, a_rt, p + 1)

            def routed_scales(p):
                pe.wait_ge(a_rt, p + 1)
                if p == 0:
                    pe.wait_ge(v_scales, 1)
                for k in range(2):
                    to = take(in_scale_bank[k])
                    for c in (2 * k, 2 * k + 1):
                        last = pe.matmul(to[:, c % 2 * 2 * P:(c % 2 + 1) * 2 * P], scales_split[:, 0, c * P:(c + 1) * P],
                                         routing_t[:, p % 2, :], start=True, stop=True)
                    last.then_inc(pe_scale, 1)
                    read_by(to, v_y, 2 * p + k + 1)

            def routed_out_scale(i):
                to = take(out_bank[1])
                pe.matmul(to[:], routing_t[:, i // 2 % 2, i % 2 * P:(i % 2 + 1) * P], scales_split[:, 1, :], start=True,
                          stop=True).then_inc(pe_os, 1)
                read_by(to, a_os, i + 1)

            def ffn_product(i):
                if i == 0:
                    pe.wait_ge(v_sign, DC)
                to = take(proj_bank[i % 2])
                toks = slice(i * P, (i + 1) * P)
                for c in range(DC):
                    if c % 2 == 0:
                        pe.wait_ge(v_ylo, i // 2 * 2 + c // 2 + 1)
                    pe.matmul(to[:], x_hi[:, c, toks], sign_w[:, c, :], start=c == 0, stop=False)
                    last = pe.matmul(to[:], x_lo[:, c, toks], sign_w[:, c, :], start=False, stop=c == DC - 1)
                last.then_inc(pe_ffn, 1)
                read_by(to, v_prod, i + 1)

            walk({"WARM": warm_up, "Q": project("Q", (wq_hi, wq_lo), (x_hi, x_lo)), "K": project("K", (wk_hi, wk_lo), (c_hi, c_lo)),
                  "V": project("V", (wv_hi, wv_lo), (c_hi, c_lo)), "X": transpose_x, "S": score, "T": transpose_probs,
                  "PV": probs_times_values, "OUT": output, "TX": ffn_transpose, "G": router, "RT": transpose_routing,
                  "R": routed_scales, "OS": routed_out_scale, "M": ffn_product})


def kernel(**inputs):
    import numpy as np
    import concourse.bacc as bacc
    from concourse.bass_utils import run_bass_kernel_spmd

    a = {k: np.asarray(v) for k, v in inputs.items()}
    per_head = lambda w: w.reshape(NH, P, DC, P).transpose(0, 3, 2, 1)
    laid = {
        "x": a["x"],
        "ctx_t": a["ctx_4096"].reshape(2, HT, DC, P).transpose(0, 3, 2, 1),
        "mask": np.ascontiguousarray(a["mask_BxSxS2_bk0"].transpose(1, 0, 2)).view(np.uint32),
        "pos_bias": a["L0_xattn_position_bias"],
        "ln_w": a["L0_xattn_ln_weight"],
        "wq": per_head(a["L0_xattn_w_q"]),
        "wk": per_head(a["L0_xattn_w_k"]),
        "wv": a["L0_xattn_w_v"].reshape(NG, VG * P, DC, P).transpose(0, 3, 2, 1),
        "wo": a["L0_xattn_w_out"].reshape(D, NPAIR, 2, P).transpose(1, 3, 2, 0),
        "ffn_w": a["L0_ffn_weight"].reshape(D, DC, P).transpose(2, 1, 0),
        "ffn_bias": a["L0_ffn_bias"],
        "gate_t": a["L0_ffn_gate_w"].reshape(E, DC, P).transpose(2, 1, 0),
        "scales": np.stack([a["L0_ffn_in_channel_scale"], a["L0_ffn_out_channel_scale"]], axis=1),
    }
    nc = bacc.Bacc("TRN2", target_bir_lowering=False, num_devices=1)
    arrays, args = {}, []
    for name, array in laid.items():
        arrays[f"in_{name}"] = np.ascontiguousarray(array)
        args.append(nc.dram_tensor(f"in_{name}", array.shape, mybir.dt.from_np(array.dtype), kind="ExternalInput").ap())
    args.append(nc.dram_tensor("out", (B, P, D), F32, kind="ExternalOutput").ap())
    xattn_ffn(nc, *args)
    return run_bass_kernel_spmd(nc, [arrays], core_ids=[0]).results[0]["out"]
```
